# Optimizing a Trainium2 kernel written in Bass

```python
import numpy as np
import jax
import jax.numpy as jnp

def _softmax(x, axis=-1):
    return jax.nn.softmax(x, axis=axis)

def _gelu(x):
    return jax.nn.gelu(x, approximate=True)

def _silu(x):
    return jax.nn.silu(x)

def _sigmoid(x):
    return jax.nn.sigmoid(x)

def _layernorm(x, axis=-1, eps=1e-05):
    m = jnp.mean(x, axis=axis, keepdims=True)
    v = jnp.var(x, axis=axis, keepdims=True)
    return (x - m) / jnp.sqrt(v + eps)

def _scatter_add(tgt, idx, src, axis=0):
    return tgt.at[idx].add(src)

def _segment_sum(src, seg, n):
    return jax.ops.segment_sum(src, seg, n)
kernel_name = 'mk_adj_ffn_d1_adj_r2_4427bb'

def setup_inputs(seed: int=0):
    np.random.seed(seed)
    _w = jnp.asarray

    def _rec_inputs():
        import jax
        import jax.numpy as jnp
        _gk = jax.random.key(seed)
        x = -0.0002928 + 1 * jax.random.normal(jax.random.fold_in(_gk, 1), (128, 128, 128), jnp.float32)
        _w = (1.0 + jnp.arange(128, dtype=jnp.float32)) ** (-0.5)
        _w = _w / _w.mean()
        _pij = jnp.clip(0.125 * _w[:, None] * _w[None, :], 0.0, 1.0)
        _a = jax.random.uniform(jax.random.fold_in(_gk, 2), (128, 128, 128)) < _pij
        _a = jnp.logical_or(_a, jnp.swapaxes(_a, -1, -2))
        _a = jnp.logical_or(_a, jnp.eye(128, dtype=bool))
        _af = _a.astype(jnp.float32)
        _af = _af * jax.random.uniform(jax.random.fold_in(_gk, 3), (128, 128, 128), jnp.float32, 0.05, 1)
        adj = _af
        return (x, adj)
    x, adj = _rec_inputs()

    def _L0_gnn_setup():
        import jax, jax.numpy as jnp
        import numpy as np
        B, N, F_IN, F_OUT = (8, 1024, 128, 128)
        key = jax.random.key(seed)
        k1, k2, k3, k4 = jax.random.split(key, 4)
        node_features = jax.random.normal(k1, (B, N, F_IN), dtype=jnp.float32)
        adj_matrix = jax.random.uniform(k2, (B, N, N), dtype=jnp.float32)
        lim = 1.0 / np.sqrt(F_IN)
        W = jax.random.uniform(k3, (F_OUT, F_IN), minval=-lim, maxval=lim, dtype=jnp.float32)
        b = jax.random.uniform(k4, (F_OUT,), minval=-lim, maxval=lim, dtype=jnp.float32)
        return {'node_features': node_features, 'adj_matrix': adj_matrix, 'W': W, 'b': b}
    _L0_gnn_all = _L0_gnn_setup()
    _L0_gnn_in = {k: v for k, v in _L0_gnn_all.items() if k in ('W', 'b')}
    del _L0_gnn_all

    def _L0_ffn_setup():
        import jax, jax.numpy as jnp
        import numpy as np
        TOP_K = 2
        LN_EPS = 1e-05
        key = jax.random.key(seed)
        ks = jax.random.split(key, 8)
        B, S, D, E, H = (16, 512, 128, 8, 512)
        x = jax.random.normal(ks[0], (B, S, D), dtype=jnp.float32)
        Wr = jax.random.normal(ks[1], (D, E), dtype=jnp.float32) * 0.1
        br = jnp.zeros((E,), dtype=jnp.float32)
        ln_g = jnp.ones((E, D), dtype=jnp.float32)
        ln_b = jnp.zeros((E, D), dtype=jnp.float32)
        W1 = jax.random.normal(ks[2], (E, D, H), dtype=jnp.float32) * (1.0 / np.sqrt(D))
        b1 = jnp.zeros((E, H), dtype=jnp.float32)
        W2 = jax.random.normal(ks[3], (E, H, D), dtype=jnp.float32) * (1.0 / np.sqrt(H))
        b2 = jnp.zeros((E, D), dtype=jnp.float32)
        return {'x': x, 'Wr': Wr, 'br': br, 'ln_g': ln_g, 'ln_b': ln_b, 'W1': W1, 'b1': b1, 'W2': W2, 'b2': b2}
    _L0_ffn_all = _L0_ffn_setup()
    _L0_ffn_in = {k: v for k, v in _L0_ffn_all.items() if k in ('Wr', 'br', 'ln_g', 'ln_b', 'W1', 'b1', 'W2', 'b2')}
    del _L0_ffn_all
    return {'x': x, 'adj': adj, 'L0_gnn_W': _L0_gnn_in['W'], 'L0_gnn_b': _L0_gnn_in['b'], 'L0_ffn_Wr': _L0_ffn_in['Wr'], 'L0_ffn_br': _L0_ffn_in['br'], 'L0_ffn_ln_g': _L0_ffn_in['ln_g'], 'L0_ffn_ln_b': _L0_ffn_in['ln_b'], 'L0_ffn_W1': _L0_ffn_in['W1'], 'L0_ffn_b1': _L0_ffn_in['b1'], 'L0_ffn_W2': _L0_ffn_in['W2'], 'L0_ffn_b2': _L0_ffn_in['b2']}

def reference(x, adj, L0_gnn_W, L0_gnn_b, L0_ffn_Wr, L0_ffn_br, L0_ffn_ln_g, L0_ffn_ln_b, L0_ffn_W1, L0_ffn_b1, L0_ffn_W2, L0_ffn_b2):
    import jax
    import jax.numpy as jnp

    def _L0_gnn_ref(node_features, adj_matrix, W, b):
        import jax, jax.numpy as jnp
        import numpy as np
        B, N, F_IN, F_OUT = (8, 1024, 128, 128)
        degree = jnp.sum(adj_matrix, axis=-1)
        d_inv_sqrt = jnp.power(degree, -0.5)
        d_inv_sqrt = jnp.where(jnp.isinf(d_inv_sqrt), 0.0, d_inv_sqrt)
        norm_adj = adj_matrix * d_inv_sqrt[:, :, None] * d_inv_sqrt[:, None, :]
        transformed = jnp.einsum('bnf,of->bno', node_features, W) + b
        output = jnp.einsum('bnm,bmo->bno', norm_adj, transformed)
        return jax.nn.relu(output)

    def _L0_ffn_ref(x, Wr, br, ln_g, ln_b, W1, b1, W2, b2):
        import jax, jax.numpy as jnp
        import numpy as np
        TOP_K = 2
        LN_EPS = 1e-05
        B, S, D = x.shape
        N = B * S
        xt = x.reshape(N, D)
        logits = xt @ Wr + br
        probs = jax.nn.softmax(logits, axis=-1)
        top_p, top_idx = jax.lax.top_k(probs, TOP_K)
        weights = top_p / top_p.sum(axis=-1, keepdims=True)
        mu = xt.mean(axis=-1, keepdims=True)
        var = ((xt - mu) ** 2).mean(axis=-1, keepdims=True)
        xn = (xt - mu) * jax.lax.rsqrt(var + LN_EPS)
        xe = xn[None, :, :] * ln_g[:, None, :] + ln_b[:, None, :]
        h = jax.nn.gelu(jnp.einsum('end,edh->enh', xe, W1) + b1[:, None, :], approximate=False)
        y = jnp.einsum('enh,ehd->end', h, W2) + b2[:, None, :]
        y_tok = jnp.transpose(y, (1, 0, 2))
        sel = jnp.take_along_axis(y_tok, top_idx[:, :, None], axis=1)
        out = (weights[:, :, None] * sel).sum(axis=1)
        return out.reshape(B, S, D)
    x = x + _L0_gnn_ref(_layernorm(x, axis=-1), adj, L0_gnn_W, L0_gnn_b)
    x = x + _L0_ffn_ref(_layernorm(x, axis=-1), L0_ffn_Wr, L0_ffn_br, L0_ffn_ln_g, L0_ffn_ln_b, L0_ffn_W1, L0_ffn_b1, L0_ffn_W2, L0_ffn_b2)
    return x

_drawn_inputs = setup_inputs


def setup_inputs(seed=0):
    import zlib

    import numpy as np

    out = dict(_drawn_inputs(seed))
    spreads = {'L0_ffn_br': (0.0, 0.1),
     'L0_ffn_ln_g': (1.0, 0.2),
     'L0_ffn_ln_b': (0.0, 0.1),
     'L0_ffn_b1': (0.0, 0.1),
     'L0_ffn_b2': (0.0, 0.1)}
    factors = {}
    for name, (base, spread) in spreads.items():
        noise = np.random.default_rng([zlib.crc32(name.encode()), seed]).standard_normal(out[name].shape)
        drawn = base * np.exp(spread * noise) if base else spread * noise
        out[name] = jnp.asarray(drawn.astype(out[name].dtype))
    for name, factor in factors.items():
        out[name] = (out[name] * factor).astype(out[name].dtype)
    return out
```

```python
from contextlib import ExitStack

import concourse.bass as bass
from concourse import mybir

F32, F16, BF16 = mybir.dt.float32, mybir.dt.float16, mybir.dt.bfloat16
I32, U32 = mybir.dt.int32, mybir.dt.uint32
ALU = mybir.AluOpType
ACT = mybir.ActivationFunctionType
AX = mybir.AxisListType

P = 128
EPS = 1e-5
TINY = 1.2e-38
WSCALE = 64.0
RING = 4
GPU = 4
WB = 16


def ge(eng, sem, count):
    if not isinstance(count, int) or count > 0:
        eng.wait_ge(sem, count)


def steps(eng, units, last_stage, step, after_first=None):
    head, total = 2 * RING, units + last_stage

    def peeled(t):
        step(t // RING, t % RING, [0 <= t - s < units for s in range(last_stage + 1)])

    for t in range(head):
        peeled(t)
        if t == RING - 1 and after_first:
            after_first()
    with eng.Fori(head // RING, units // RING) as i:
        for k in range(RING):
            step(i, k, [True] * (last_stage + 1))
    for t in range(units // RING * RING, total):
        peeled(t)


def unit_of(i, k, stage):
    return i + (k - stage) // RING, (k - stage) % RING


def pick(ap, u):
    return ap[bass.ds(u, 1)].rearrange("o n c d -> (o n) c d")


def gnn_moe(nc, x, adj, gnn_w, gnn_b, wr, br, ln_g, ln_b, w1, b1, w2, b2, out):
    B, N, D = x.shape
    E, _, H = w1.shape
    HJ = H // P
    TOKENS = B * N
    UNITS = B // GPU
    UW = GPU * P
    PAIRS = E * (E - 1) // 2
    TILES = (TOKENS + PAIRS * (P - 1)) // P
    TILES += -TILES % RING
    ROW = 2 * D + 2
    PAD_ROW = TOKENS
    ROUNDS = B // WB
    assert N == P and D == P and B == P and UNITS % RING == 0

    rows = nc.dram_tensor("token_rows", [TOKENS + 1, ROW], F32).ap()
    x_u = x.rearrange("(u c) n d -> u n c d", c=GPU)
    adj_u = adj.rearrange("(u c) n m -> u n c m", c=GPU)
    rows_u = rows[0:TOKENS, :].rearrange("(u c n) f -> u n c f", c=GPU, n=P)
    rows_c = rows[0:TOKENS, :].rearrange("(c n) f -> n c f", n=P)
    out_rows = out.rearrange("b n d -> (b n) d")

    with ExitStack() as ctx:
        def sb(name, shape, dt=F32, where=ctx):
            return where.enter_context(nc.sbuf_tensor(name, shape, dt))

        def sem(name):
            return ctx.enter_context(nc.semaphore(name))

        ident = sb("ident", [P, P])
        before = sb("before", [P, P], BF16)
        ones_b = sb("ones_b", [P, P], BF16)
        ones_h = sb("ones_h", [P, P], F16)
        neg_half = sb("neg_half", [P, 2 * GPU])
        iota_e = sb("iota_e", [P, E])
        iota_q = sb("iota_q", [P, PAIRS])
        iota_lo = sb("iota_lo", [P, P], F16)
        iota_hi = sb("iota_hi", [P, TILES], F16)
        number = sb("number", [P, WB])
        round_base = sb("round_base", [P, ROUNDS])
        gnn_w_in = sb("gnn_w_in", [P, P])
        gnn_wT = sb("gnn_wT", [P, P])
        gnn_b_row = sb("gnn_b_row", [1, P])
        wr_sb = sb("wr_sb", [P, E])
        br_all = sb("br_all", [P, E])
        ln_in = sb("ln_in", [2 * E, P])
        lnT = sb("lnT", [P, 2 * E])
        b1_in = sb("b1_in", [E * HJ, P])
        b1T = sb("b1T", [P, E * HJ])
        b2_in = sb("b2_in", [P, E * D])
        b2_pad = sb("b2_pad", [P, E, D], F16)
        w1_f = sb("w1_f", [P, E, H])
        w2_f = sb("w2_f", [P, E, H])
        w_s = sb("w_s", [P, E, H])
        w1_s = sb("w1_s", [P, E, 2, H], F16)
        w2_s = sb("w2_s", [P, E, 2, H], F16)

        b2_high = sb("b2_high", [P, E * D], F16)
        zero_row = sb("zero_row", [1, ROW])
        keep = sb("keep", [P, PAIRS, B], BF16)
        iota_t = sb("iota_t", [1, TILES])
        a_ends = sb("a_ends", [1, E - 1])

        list_f = sb("list_f", [P, TILES])

        logits = sb("logits", [P, B, E])
        list_i = sb("list_i", [P, TILES], I32)
        table = sb("table", [1, 2, TILES], I32)

        with ExitStack() as a:
            x_in = sb("x_in", [P, RING, GPU, P], where=a)
            adj_in = sb("adj_in", [P, RING, GPU, P], where=a)
            pair_rows = sb("pair_rows", [P, RING, GPU, 2 * D], where=a)
            adjT = sb("adjT", [P, 2, UW], where=a)
            xd = sb("xd", [P, 2, GPU, P], where=a)
            aggT = sb("aggT", [P, 2, UW], where=a)
            degsum = sb("degsum", [1, 2, UW], where=a)
            relu = sb("relu", [P, 2, GPU, P], where=a)
            xnT = sb("xnT", [P, 2, UW], where=a)
            stats = sb("stats", [P, 2, GPU, 6], where=a)
            mv1 = sb("mv1", [P, RING, GPU, 2], where=a)
            mv2 = sb("mv2", [P, RING, GPU, 2], where=a)
            stats2 = sb("stats2", [P, 2, GPU, 6], where=a)
            deg = sb("deg", [P, 2, GPU], where=a)
            z1 = sb("z1", [P, 2, 2 * GPU], where=a)
            y1 = sb("y1", [P, 2, 2 * GPU], where=a)
            dinv = sb("dinv", [P, RING, GPU], where=a)
            xs = sb("xs", [P, 2, GPU], where=a)
            z2 = sb("z2", [P, 2, 2 * GPU], where=a)
            y2 = sb("y2", [P, 2, 2 * GPU], where=a)
            rt = sb("rt", [P, 2, GPU], where=a)
            ratio = sb("ratio", [P, RING, GPU], where=a)
        wab = sb("wab", [P, B, 2])
        wide = [sb(f"r_wide{n}", [P, B, E]) for n in range(2)]
        sm = {n: sb(f"r_{n}", [P, B]) for n in
              ("m1", "m2", "i0", "i1", "e", "rden", "w1", "w2", "first", "t1", "t2", "a", "b", "q",
               "slot", "lo", "hi")}
        slot_i = sb("slot_i", [P, B], I32)
        part_i = sb("part_i", [P, B], I32)
        onehot = sb("onehot", [P, PAIRS, B], BF16)
        rank = sb("rank", [P, PAIRS, B])
        row_count = sb("row_count", [P, PAIRS], BF16)
        tiles_i = sb("tiles_i", [P, PAIRS], I32)
        tiles_f = sb("tiles_f", [P, PAIRS])
        tiles_end = sb("tiles_end", [P, PAIRS])
        slot_base = sb("slot_base", [P, PAIRS])
        lo_hot = sb("lo_hot", [P, 8, P], F16)
        hi_hot = sb("hi_hot", [P, 8, TILES], F16)
        list_t = sb("list_t", [P, TILES])
        tq = sb("tq", [1, TILES, PAIRS], BF16)
        q_of = sb("q_of", [1, TILES])
        ta = sb("ta", [1, TILES])
        tb = sb("tb", [1, TILES])

        tile_row = sb("tile_row", [P, RING, ROW])
        get_idx = sb("get_idx", [P, RING], I32)
        put_idx = sb("put_idx", [P, RING], I32)
        xh = sb("xh", [P, 2, P], F16)
        xl = sb("xl", [P, 2, P], F16)
        hid = sb("hid", [P, 2, H])
        hid_h = sb("hid_h", [P, 2, 2, H], F16)
        hid_l = sb("hid_l", [P, 2, 2, H], F16)
        part = sb("part", [P, 2, D])
        result = sb("result", [P, 2, D])

        bank = [ctx.enter_context(nc.psum_tensor(f"bank{n}", [P, 512], F32)) for n in range(8)]

        x_ld = [sem(f"x_ld{r}") for r in range(RING)]
        adj_ld = [sem(f"adj_ld{r}") for r in range(RING)]
        rows_st = [sem(f"rows_st{r}") for r in range(RING)]
        small_ld, w1_ld, w2_ld = sem("small_ld"), sem("w1_ld"), sem("w2_ld")
        pad_st, wab_st = sem("pad_st"), sem("wab_st")
        filled, consts = sem("filled"), sem("consts")
        prep_ps, prep_ok, b2_ok = sem("prep_ps"), sem("prep_ok"), sem("b2_ok")
        (stats_ok, mv1_ok, z1_ok, y1_ok, dinv_ok, xs_ok, xd_ok, adjT_ps, adjT_ok, agg_ps, agg_ok,
         dsum_ps, dsum_ok, gnn_ps, relu_ok, x1_ok, stats2_ok, mv2_ok, ve_ok, z2_ok, y2_ok,
         xn_ok, rt_ok, ratio_ok, xnT_ps, xnT_ok, lg_ps, lg_ok) = (sem("a_" + n) for n in (
             "stats", "mv1", "z1", "y1", "dinv", "xs", "xd", "adjT_ps", "adjT", "agg_ps", "agg",
             "dsum_ps", "dsum", "gnn_ps", "relu", "x1", "stats2", "mv2", "ve", "z2", "y2", "xn",
             "rt", "ratio", "xnT_ps", "xnT", "lg_ps", "lg"))
        link, gap_ok, exp_ok, wab_ok, count_ok, prefix_ps = (sem("r_" + n) for n in (
            "link", "gap", "exp", "wab", "count", "prefix_ps"))
        hot_ok, acc_ps, acc_used, list_sum, list_ok, table_ok, shift_ps = (sem("r_" + n) for n in (
            "hot", "acc_ps", "acc_used", "list_sum", "list", "table", "shift_ps"))
        scaled_ok, high_ok, low_ok = sem("w_scaled"), sem("w_high"), sem("w_low")
        row_ld = [sem(f"row_ld{r}") for r in range(RING)]
        (get_idx_ok, put_idx_ok, xT_ps, xh_ok, xl_ok, z_ps, hid_ok, hh_ok, hl_ok, y_ps, part_ok,
         res_ok, out_st) = (sem("b_" + n) for n in (
             "get_idx", "put_idx", "xT_ps", "xh", "xl", "z_ps", "hid", "hh", "hl", "y_ps", "part",
             "res", "out_st"))

        SMALL = 9
        FILLS, CONSTS = 7, 13
        block = ctx.enter_context(nc.Block())

        @block.sync
        def _(sp):
            def small(dst, src):
                sp.dma_start(dst, src).then_inc(small_ld, 16)

            small(gnn_w_in[:, :], gnn_w)
            small(gnn_b_row[:, :], gnn_b.rearrange("(a d) -> a d", a=1))
            small(wr_sb[:, :], wr)
            small(ln_in[0:E, :], ln_g)
            small(ln_in[E:2 * E, :], ln_b)
            small(b1_in[:, :], b1.rearrange("e (j p) -> (e j) p", p=P))
            small(b2_in[0:1, :], b2.rearrange("(a e) d -> a (e d)", a=1))
            small(b2_in[32:33, :], b2.rearrange("(a e) d -> a (e d)", a=1))
            small(br_all[:, :], br.partition_broadcast(P))

            def step(i, k, active):
                if active[0]:
                    m, r = unit_of(i, k, 0)
                    u = RING * m + r
                    ge(sp, x1_ok, u - RING + 1)
                    sp.dma_start(x_in[:, r], pick(x_u, u)).then_inc(x_ld[r], 16)
                    ge(sp, z1_ok, u - RING + 1)
                    ge(sp, adjT_ps, u - RING + 1)
                    sp.dma_start(adj_in[:, r], pick(adj_u, u)).then_inc(adj_ld[r], 16)
                if active[4]:
                    m, r = unit_of(i, k, 4)
                    u = RING * m + r
                    ge(sp, xn_ok, u + 1)
                    sp.dma_start(pick(rows_u, u)[:, :, 0:2 * D], pair_rows[:, r]).then_inc(rows_st[r], 16)

            def experts_weights():
                sp.dma_start(w1_f[:, :, :], w1.rearrange("e p h -> p e h")).then_inc(w1_ld, 16)
                sp.dma_start(w2_f[:, :, :].rearrange("p e (j d) -> p (e j) d", j=HJ),
                             w2.rearrange("e (j p) d -> p (e j) d", p=P)).then_inc(w2_ld, 16)

            steps(sp, UNITS, 5, step, experts_weights)
            sp.wait_ge(consts, CONSTS)
            sp.dma_start(rows[TOKENS:TOKENS + 1, :], zero_row[:, :]).then_inc(pad_st, 16)
            sp.wait_ge(wab_ok, 1)
            sp.dma_start(rows_c[:, :, 2 * D:2 * D + 2], wab[:, :, :]).then_inc(wab_st, 16)
            sp.wait_ge(pad_st, 16)
            sp.wait_ge(wab_st, 16)
            for r in range(RING):
                sp.wait_ge(rows_st[r], 16 * (UNITS // RING))
            sp.wait_ge(out_st, 16 * TILES)

        @block.gpsimd
        def _(pool):
            def fill(ap, value):
                pool.memset(ap, value).then_inc(filled, 1)

            def const(ins):
                ins.then_inc(consts, 1)

            fill(ident[:, :], 0.0)
            fill(before[:, :], 1.0)
            fill(keep[:, :, :], 1.0)
            fill(ones_b[:, :], 1.0)
            fill(ones_h[:, :], 1.0)
            fill(neg_half[:, :], -0.5)
            fill(b2_pad[:, :, :], 0.0)
            pool.wait_ge(filled, FILLS)
            const(pool.affine_select(out=ident[:, :], in_=ident[:, :], compare_op=ALU.not_equal, fill=1.0,
                                     base=0, pattern=[[-1, P]], channel_multiplier=1))
            const(pool.affine_select(out=before[:, :], in_=before[:, :], compare_op=ALU.is_gt, fill=0.0,
                                     base=0, pattern=[[1, P]], channel_multiplier=-1))
            const(pool.affine_select(out=keep[:, :, :], in_=keep[:, :, :], compare_op=ALU.is_gt, fill=0.0,
                                     base=0, pattern=[[0, PAIRS], [1, B]], channel_multiplier=0))
            for ap, pattern, base, per_row in ((iota_e, [[1, E]], -E, 0), (iota_q, [[1, PAIRS]], 0, 0),
                                               (iota_lo, [[1, P]], 0, 0), (iota_hi, [[1, TILES]], 0, 0),
                                               (number, [[P, WB]], 1, 1),
                                               (round_base, [[WB * P, ROUNDS]], 0, 0),
                                               (iota_t, [[1, TILES]], 0, 0)):
                const(pool.iota(ap[:, :], pattern=pattern, base=base, channel_multiplier=per_row,
                                allow_small_or_imprecise_dtypes=True))
            const(pool.memset(zero_row[:, :], 0.0))
            const(pool.memset(list_f[:, :], 0.0))
            for a in range(E - 1):
                end = sum(E - 1 - n for n in range(a + 1))
                last = pool.memset(a_ends[:, a:a + 1], float(end))
            const(last)

            def step(i, k, active):
                if active[0]:
                    m, r = unit_of(i, k, 0)
                    u = RING * m + r
                    ge(pool, z1_ok, u + 1)
                    ge(pool, xd_ok, u - 1)
                    pool.tensor_tensor(y1[:, r % 2], z1[:, r % 2], neg_half[:, :], ALU.pow).then_inc(y1_ok, 1)
                if active[3]:
                    m, r = unit_of(i, k, 3)
                    u = RING * m + r
                    ge(pool, z2_ok, u + 1)
                    ge(pool, xn_ok, u - 1)
                    ge(pool, ratio_ok, u - 1)
                    pool.tensor_tensor(y2[:, r % 2], z2[:, r % 2], neg_half[:, :], ALU.pow).then_inc(y2_ok, 1)
                if active[2]:
                    m, r = unit_of(i, k, 2)
                    u = RING * m + r
                    ge(pool, relu_ok, u + 1)
                    ge(pool, rows_st[r], 16 * m)
                    pool.tensor_tensor(pair_rows[:, r, :, D:2 * D], x_in[:, r], relu[:, r % 2],
                                       ALU.add).then_inc(x1_ok, 1)

            steps(pool, UNITS, 5, step)

            for n, split in enumerate((w1_s, w2_s)):
                pool.wait_ge(high_ok, n + 1)
                pool.tensor_tensor(split[:, :, 1, :], w_s[:, :, :], split[:, :, 0, :],
                                   ALU.subtract).then_inc(low_ok, 1)

            pool.wait_ge(list_ok, 1)
            pool.wait_ge(wab_st, 16)
            pool.wait_ge(pad_st, 16)
            for r in range(RING):
                pool.wait_ge(rows_st[r], 16 * (UNITS // RING))

            last_row, last_token = pool.to_reg(TOKENS), pool.to_reg(TOKENS - 1)

            def step_b(i, k, active):
                if active[1]:
                    m, r1 = unit_of(i, k, 1)
                    u1 = RING * m + r1
                    ge(pool, get_idx_ok, u1 + 1)
                    ge(pool, res_ok, u1 - RING + 1)
                if active[0]:
                    m, r = unit_of(i, k, 0)
                    u = RING * m + r
                    ge(pool, row_ld[r], 16 * m)
                    pool.tensor_copy(get_idx[:, r:r + 1], list_i[:, bass.ds(u, 1)]).then_inc(get_idx_ok, 1)
                if active[1]:
                    pool.indirect_dma_start(
                        tile_row[:, r1, :], None, rows[:, :],
                        bass.IndirectOffsetOnAxis(ap=get_idx[:, r1:r1 + 1].bitcast(U32), axis=0),
                        bounds_check=last_row, oob_is_err=False).then_inc(row_ld[r1], 16)
                if active[5]:
                    m, r5 = unit_of(i, k, 5)
                    u5 = RING * m + r5
                    ge(pool, out_st, 16 * u5)
                    ge(pool, res_ok, u5 + 1)
                    ge(pool, put_idx_ok, u5 + 1)
                if active[4]:
                    m, r = unit_of(i, k, 4)
                    u = RING * m + r
                    ge(pool, out_st, 16 * (u - RING + 1))
                    pool.tensor_copy(put_idx[:, r:r + 1], list_i[:, bass.ds(u, 1)]).then_inc(put_idx_ok, 1)
                if active[5]:
                    pool.indirect_dma_start(
                        out_rows, bass.IndirectOffsetOnAxis(ap=put_idx[:, r5:r5 + 1].bitcast(U32), axis=0),
                        result[:, r5 % 2, :], None,
                        bounds_check=last_token, oob_is_err=False).then_inc(out_st, 16)

            steps(pool, TILES, 5, step_b)

        @block.scalar
        def _(act):
            def step(i, k, active):
                if active[0]:
                    m, r = unit_of(i, k, 0)
                    u = RING * m + r
                    ge(act, adjT_ps, u + 1)
                    ge(act, agg_ps, u - 1)
                    ge(act, dsum_ps, u - 1)
                    act.activation(adjT[:, r % 2], bank[r % 2][:, :], ACT.Copy).then_inc(adjT_ok, 1)
                if active[2]:
                    m, r = unit_of(i, k, 2)
                    u = RING * m + r
                    ge(act, gnn_ps, u + 1)
                    ge(act, x1_ok, u - 1)
                    for c in range(GPU):
                        last = act.activation(relu[:, r % 2, c], bank[4 + r % 2][:, c * P:(c + 1) * P],
                                              ACT.Relu, scale=dinv[:, r, c:c + 1])
                    last.then_inc(relu_ok, 1)
                if active[4]:
                    m, r = unit_of(i, k, 4)
                    u = RING * m + r
                    ge(act, xnT_ps, u + 1)
                    ge(act, lg_ps, u - 1)
                    act.activation(xnT[:, r % 2], bank[6][:, :], ACT.Copy).then_inc(xnT_ok, 1)
                if active[1]:
                    m, r = unit_of(i, k, 1)
                    u = RING * m + r
                    ge(act, agg_ps, u + 1)
                    ge(act, gnn_ps, u - 1)
                    act.activation(aggT[:, r % 2], bank[2][:, :], ACT.Copy).then_inc(agg_ok, 1)
                    ge(act, dsum_ps, u + 1)
                    act.activation(degsum[:, r % 2], bank[3][0:1, :], ACT.Copy).then_inc(dsum_ok, 1)

            steps(act, UNITS, 5, step)

            act.wait_ge(w1_ld, 16)
            for e in range(E):
                last = act.activation(w_s[:, e, :], w1_f[:, e, :], ACT.Copy, scale=lnT[:, e:e + 1])
            last.then_inc(scaled_ok, 1)
            act.wait_ge(scaled_ok, 1)
            act.activation(w1_s[:, :, 0, :], w_s[:, :, :], ACT.Copy).then_inc(high_ok, 1)
            act.wait_ge(gap_ok, 1)
            act.activation(sm["e"][:, :], sm["t1"][:, :], ACT.Exp).then_inc(exp_ok, 1)
            act.wait_ge(low_ok, 1)
            act.wait_ge(w2_ld, 16)
            act.activation(w_s[:, :, :], w2_f[:, :, :], ACT.Copy, scale=WSCALE).then_inc(scaled_ok, 1)
            act.wait_ge(scaled_ok, 2)
            act.activation(w2_s[:, :, 0, :], w_s[:, :, :], ACT.Copy).then_inc(high_ok, 1)
            act.wait_ge(table_ok, 2)

            def step_b(i, k, active):
                if active[2]:
                    m, r = unit_of(i, k, 2)
                    u = RING * m + r
                    ge(act, xT_ps, u + 1)
                    ge(act, z_ps, 2 * u - 2)
                    act.activation(xh[:, r % 2], bank[4 + r % 2][:, 0:P], ACT.Copy).then_inc(xh_ok, 1)
                if active[3]:
                    m, r = unit_of(i, k, 3)
                    u = RING * m + r
                    for n in range(2):
                        e = act.value_load(table[0:1, n, bass.ds(u, 1)], min_val=0, max_val=E - 1)
                        ge(act, z_ps, 2 * u + n + 1)
                        ge(act, hl_ok, 2 * u + n - 1)
                        for j in range(HJ):
                            last = act.activation(hid[:, n, j * P:(j + 1) * P],
                                                  bank[2 * (r % 2) + n][:, j * P:(j + 1) * P], ACT.Gelu,
                                                  bias=b1T[:, bass.ds(HJ * e + j, 1)], scale=1.0 / WSCALE)
                        last.then_inc(hid_ok, 1)

            steps(act, TILES, 5, step_b)

        @block.tensor
        def _(pe):
            pe.wait_ge(small_ld, 16 * SMALL)
            pe.wait_ge(consts, 1)
            pe.transpose(bank[0][:, 0:P], gnn_w_in[:, :], ident[:, :])
            pe.transpose(bank[0][:, P:P + 2 * E], ln_in[:, :], ident[0:2 * E, 0:2 * E])
            pe.transpose(bank[0][:, 2 * P:2 * P + E * HJ], b1_in[:, :],
                         ident[0:E * HJ, 0:E * HJ]).then_inc(prep_ps, 1)
            pe.wait_ge(prep_ok, 3)

            def step(i, k, active):
                if active[0]:
                    m, r = unit_of(i, k, 0)
                    u = RING * m + r
                    ge(pe, adj_ld[r], 16 * m + 16)
                    ge(pe, adjT_ok, u - 1)
                    for c in range(GPU):
                        last = pe.transpose(bank[r % 2][:, c * P:(c + 1) * P], adj_in[:, r, c], ident[:, :])
                    last.then_inc(adjT_ps, 1)
                if active[2]:
                    m, r = unit_of(i, k, 2)
                    u = RING * m + r
                    ge(pe, agg_ok, u + 1)
                    ge(pe, dsum_ok, u + 1)
                    ge(pe, relu_ok, u - 1)
                    for c in range(GPU):
                        o = bank[4 + r % 2][:, c * P:(c + 1) * P]
                        pe.matmul(o, aggT[:, r % 2, c * P:(c + 1) * P], gnn_wT[:, :], start=True, stop=False)
                        last = pe.matmul(o, degsum[:, r % 2, c * P:(c + 1) * P], gnn_b_row[:, :],
                                         start=False, stop=True)
                    last.then_inc(gnn_ps, 1)
                if active[5]:
                    m, r = unit_of(i, k, 5)
                    u = RING * m + r
                    ge(pe, xnT_ok, u + 1)
                    ge(pe, lg_ok, u)
                    for c in range(GPU):
                        last = pe.matmul(bank[7][:, c * E:(c + 1) * E], xnT[:, r % 2, c * P:(c + 1) * P],
                                         wr_sb[:, :], start=True, stop=True)
                    last.then_inc(lg_ps, 1)
                if active[4]:
                    m, r = unit_of(i, k, 4)
                    u = RING * m + r
                    ge(pe, xn_ok, u + 1)
                    ge(pe, xnT_ok, u)
                    for c in range(GPU):
                        last = pe.transpose(bank[6][:, c * P:(c + 1) * P], pair_rows[:, r, c, 0:D], ident[:, :])
                    last.then_inc(xnT_ps, 1)
                if active[1]:
                    m, r = unit_of(i, k, 1)
                    u = RING * m + r
                    ge(pe, xd_ok, u + 1)
                    ge(pe, adjT_ok, u + 1)
                    ge(pe, agg_ok, u)
                    for c in range(GPU):
                        last = pe.matmul(bank[2][:, c * P:(c + 1) * P], xd[:, r % 2, c],
                                         adjT[:, r % 2, c * P:(c + 1) * P], start=True, stop=True)
                    last.then_inc(agg_ps, 1)
                    ge(pe, dsum_ok, u)
                    for c in range(GPU):
                        last = pe.matmul(bank[3][0:1, c * P:(c + 1) * P], dinv[:, r, c:c + 1],
                                         adjT[:, r % 2, c * P:(c + 1) * P], start=True, stop=True)
                    last.then_inc(dsum_ps, 1)

            steps(pe, UNITS, 5, step)

            pe.wait_ge(w1_ld, 16)
            for n in range(E * HJ):
                e, j = divmod(n, HJ)
                last = pe.matmul(bank[0][:, n:n + 1], w1_f[:, e, j * P:(j + 1) * P], lnT[:, E + e:E + e + 1],
                                 start=True, stop=True)
            last.then_inc(shift_ps, 1)
            pe.wait_ge(count_ok, 1)
            pe.matmul(bank[1][:, 0:PAIRS], before[:, :], row_count[:, :], start=True, stop=True)
            pe.matmul(bank[2][:, 0:PAIRS], ones_b[:, :], row_count[:, :], start=True,
                      stop=True).then_inc(prefix_ps, 1)
            with pe.Fori(0, ROUNDS) as n:
                pe.wait_ge(acc_used, n + 1)
                for c in range(WB):
                    pe.wait_ge(hot_ok, WB * n + (c + 1))
                    last = pe.matmul(bank[3][:, 0:TILES], lo_hot[:, c % 8], hi_hot[:, c % 8],
                                     start=(c == 0), stop=(c == WB - 1))
                    last.then_inc(acc_ps, 1)

            pe.wait_ge(low_ok, 2)
            pe.wait_ge(b2_ok, 2)
            pe.wait_ge(table_ok, 2)
            w1_at = w1_s[:, :, :, :].rearrange("p e l h -> p (e l h)")
            w2_at = w2_s[:, :, :, :].rearrange("p e l h -> p (e l h)")
            b2_at = b2_pad[:, :, :].rearrange("p e d -> p (e d)")

            def step_b(i, k, active):
                if active[2]:
                    m, r = unit_of(i, k, 2)
                    u = RING * m + r
                    ge(pe, row_ld[r], 16 * m + 16)
                    ge(pe, xh_ok, u - 1)
                    ge(pe, xl_ok, u - 1)
                    pe.transpose(bank[4 + r % 2][:, 0:P], tile_row[:, r, 0:D], ident[:, :]).then_inc(xT_ps, 1)
                if active[3]:
                    m, r = unit_of(i, k, 3)
                    u = RING * m + r
                    for n in range(2):
                        e = pe.value_load(table[0:1, n, bass.ds(u, 1)], min_val=0, max_val=E - 1)
                        at = pe.snap(e * (2 * H))
                        ge(pe, xh_ok, u + 1)
                        ge(pe, xl_ok, u + 1)
                        ge(pe, hid_ok, 2 * u + n - 3)
                        for j in range(HJ):
                            o = bank[2 * (r % 2) + n][:, j * P:(j + 1) * P]
                            high = w1_at[:, bass.ds(at + j * P, P)]
                            pe.matmul(o, high, xh[:, r % 2], start=True, stop=False)
                            pe.matmul(o, high, xl[:, r % 2], start=False, stop=False)
                            last = pe.matmul(o, w1_at[:, bass.ds(at + (H + j * P), P)], xh[:, r % 2],
                                             start=False, stop=True)
                        last.then_inc(z_ps, 1)
                if active[4]:
                    m, r = unit_of(i, k, 4)
                    u = RING * m + r
                    for n in range(2):
                        e = pe.value_load(table[0:1, n, bass.ds(u, 1)], min_val=0, max_val=E - 1)
                        at = pe.snap(e * (2 * H))
                        ge(pe, res_ok, u - 1)
                        ge(pe, hl_ok, 2 * u + n + 1)
                        o = bank[6 + r % 2][:, n * D:(n + 1) * D]
                        pe.matmul(o, ones_h[:, :], b2_at[:, bass.ds(e * D, D)], start=True, stop=False)
                        for j in range(HJ):
                            hh, hl = (s[:, r % 2, n, j * P:(j + 1) * P] for s in (hid_h, hid_l))
                            high = w2_at[:, bass.ds(at + j * P, P)]
                            pe.matmul(o, hh, high, start=False, stop=False)
                            pe.matmul(o, hh, w2_at[:, bass.ds(at + (H + j * P), P)], start=False, stop=False)
                            last = pe.matmul(o, hl, high, start=False, stop=(j == HJ - 1))
                    last.then_inc(y_ps, 1)

            steps(pe, TILES, 5, step_b)

        @block.vector
        def _(dve):
            dve.wait_ge(prep_ps, 1)
            dve.tensor_copy(gnn_wT[:, :], bank[0][:, 0:P]).then_inc(prep_ok, 1)
            dve.tensor_scalar(lnT[:, 0:E], bank[0][:, P:P + E], WSCALE, None, ALU.mult)
            dve.tensor_copy(lnT[:, E:2 * E], bank[0][:, P + E:P + 2 * E]).then_inc(prep_ok, 1)
            dve.tensor_copy(b1T[:, :], bank[0][:, 2 * P:2 * P + E * HJ]).then_inc(prep_ok, 1)
            dve.wait_ge(consts, 1)
            dve.tensor_scalar(b2_pad[0:1].rearrange("p e d -> p (e d)"), b2_in[0:1, :], WSCALE, None, ALU.mult)
            dve.tensor_scalar(b2_high[32:33, :], b2_in[32:33, :], WSCALE, None, ALU.mult).then_inc(b2_ok, 1)
            dve.wait_ge(b2_ok, 1)
            dve.scalar_tensor_tensor(b2_pad[32:33].rearrange("p e d -> p (e d)"), b2_in[32:33, :], WSCALE,
                                     b2_high[32:33, :], ALU.mult, ALU.subtract).then_inc(b2_ok, 1)

            def step(i, k, active):
                if active[1]:
                    m, r = unit_of(i, k, 1)
                    u = RING * m + r
                    ge(dve, y1_ok, u + 1)
                    ge(dve, relu_ok, u - RING + 1)
                    dve.scalar_tensor_tensor(dinv[:, r], deg[:, r % 2], 0.0, y1[:, r % 2, GPU:], ALU.is_gt,
                                             ALU.mult).then_inc(dinv_ok, 1)
                    ge(dve, dinv_ok, u + 1)
                    dve.tensor_tensor(xs[:, r % 2], y1[:, r % 2, 0:GPU], dinv[:, r], ALU.mult).then_inc(xs_ok, 1)
                    ge(dve, xs_ok, u + 1)
                    ge(dve, agg_ps, u - 1)
                    for c in range(GPU):
                        last = dve.tensor_scalar(xd[:, r % 2, c], x_in[:, r, c], mv1[:, r, c, 0:1],
                                                 xs[:, r % 2, c:c + 1], ALU.subtract, ALU.mult)
                    last.then_inc(xd_ok, 1)
                if active[0]:
                    m, r = unit_of(i, k, 0)
                    u = RING * m + r
                    ge(dve, x_ld[r], 16 * m + 16)
                    for c in range(GPU):
                        last = dve.bn_stats(stats[:, r % 2, c], x_in[:, r, c])
                    last.then_inc(stats_ok, 1)
                    ge(dve, adj_ld[r], 16 * m + 16)
                    ge(dve, stats_ok, u + 1)
                    dve.tensor_reduce(deg[:, r % 2], adj_in[:, r], AX.X, ALU.add)
                    for c in range(GPU):
                        last = dve.bn_aggr(mv1[:, r, c], stats[:, r % 2, c])
                    last.then_inc(mv1_ok, 1)
                    ge(dve, mv1_ok, u + 1)
                    ge(dve, y1_ok, u - 1)
                    dve.tensor_scalar(z1[:, r % 2, GPU:], deg[:, r % 2], TINY, None, ALU.max)
                    dve.tensor_scalar(z1[:, r % 2, 0:GPU], mv1[:, r, :, 1], EPS, None, ALU.add).then_inc(z1_ok, 1)
                if active[4]:
                    m, r = unit_of(i, k, 4)
                    u = RING * m + r
                    ge(dve, y2_ok, u + 1)
                    for c in range(GPU):
                        last = dve.tensor_scalar(pair_rows[:, r, c, 0:D], pair_rows[:, r, c, D:2 * D],
                                                 mv2[:, r, c, 0:1], y2[:, r % 2, GPU + c:GPU + c + 1],
                                                 ALU.subtract, ALU.mult)
                    last.then_inc(xn_ok, 1)
                    dve.tensor_tensor(rt[:, r % 2], z2[:, r % 2, GPU:], y2[:, r % 2, GPU:], ALU.mult).then_inc(rt_ok, 1)
                    ge(dve, rt_ok, u + 1)
                    dve.tensor_tensor(ratio[:, r], rt[:, r % 2], y2[:, r % 2, 0:GPU], ALU.mult).then_inc(ratio_ok, 1)
                if active[3]:
                    m, r = unit_of(i, k, 3)
                    u = RING * m + r
                    ge(dve, x1_ok, u + 1)
                    for c in range(GPU):
                        last = dve.bn_stats(stats2[:, r % 2, c], pair_rows[:, r, c, D:2 * D])
                    last.then_inc(stats2_ok, 1)
                    ge(dve, stats2_ok, u + 1)
                if active[5]:
                    m, r5 = unit_of(i, k, 5)
                    u5 = RING * m + r5
                    ge(dve, lg_ps, u5 + 1)
                    ge(dve, ratio_ok, u5 + 1)
                    dve.tensor_tensor(logits[:, bass.ds(GPU * u5, GPU), :],
                                      bank[7][:, 0:GPU * E].rearrange("p (c e) -> p c e", e=E),
                                      ratio[:, r5].unsqueeze(2).to_broadcast([P, GPU, E]),
                                      ALU.mult).then_inc(lg_ok, 1)
                if active[3]:
                    for c in range(GPU):
                        last = dve.bn_aggr(mv2[:, r, c], stats2[:, r % 2, c])
                    last.then_inc(mv2_ok, 1)
                    ge(dve, mv2_ok, u + 1)
                    dve.tensor_scalar(z2[:, r % 2, 0:GPU], mv2[:, r, :, 1], EPS, None, ALU.add).then_inc(ve_ok, 1)
                    ge(dve, ve_ok, u + 1)
                    dve.scalar_tensor_tensor(z2[:, r % 2, GPU:], z2[:, r % 2, 0:GPU], EPS, mv2[:, r, :, 1],
                                             ALU.mult, ALU.add).then_inc(z2_ok, 1)

            steps(dve, UNITS, 5, step)

            made = [0]

            def then(ins):
                made[0] += 1
                ins.then_inc(link, 1)
                dve.wait_ge(link, made[0])

            for r in range(RING):
                dve.wait_ge(rows_st[r], 16 * (UNITS // RING))
            dve.wait_ge(consts, CONSTS)
            dve.wait_ge(lg_ok, UNITS)
            big0, big1 = (t[:, :, :] for t in wide)
            per_e = lambda ap: ap[:, :].unsqueeze(2).to_broadcast([P, B, E])
            per_c = lambda ap: ap[:, :].unsqueeze(1).to_broadcast([P, B, E])
            s = {n: t[:, :] for n, t in sm.items()}
            lg = logits[:, :, :]
            then(dve.tensor_tensor(lg, lg, per_c(br_all), ALU.add))
            then(dve.tensor_reduce(s["m1"], lg, AX.X, ALU.max))
            then(dve.tensor_tensor(big0, lg, per_e(sm["m1"]), ALU.is_equal))
            then(dve.tensor_tensor(big0, big0, per_c(iota_e), ALU.mult))
            then(dve.tensor_reduce(s["i0"], big0, AX.X, ALU.min))
            then(dve.tensor_tensor(big0, per_e(sm["i0"]), per_c(iota_e), ALU.is_equal))
            then(dve.scalar_tensor_tensor(big1, big0, -3e38, lg, ALU.mult, ALU.add))
            then(dve.tensor_reduce(s["w2"], big1, AX.X, ALU.max))
            dve.tensor_tensor(s["t1"], s["w2"], s["m1"], ALU.subtract).then_inc(gap_ok, 1)
            then(dve.tensor_tensor(big0, big1, per_e(sm["w2"]), ALU.is_equal))
            then(dve.tensor_tensor(big0, big0, per_c(iota_e), ALU.mult))
            then(dve.tensor_reduce(s["i1"], big0, AX.X, ALU.min))
            dve.wait_ge(exp_ok, 1)
            then(dve.tensor_scalar(s["t2"], s["e"], 1.0, None, ALU.add))
            then(dve.reciprocal(s["rden"], s["t2"]))
            dve.tensor_scalar(s["w1"], s["rden"], 1.0 / WSCALE, None, ALU.mult)
            then(dve.scalar_tensor_tensor(s["w2"], s["e"], 1.0 / WSCALE, s["rden"], ALU.mult, ALU.mult))
            dve.tensor_tensor(s["first"], s["i0"], s["i1"], ALU.is_lt)
            dve.tensor_tensor(s["a"], s["i0"], s["i1"], ALU.min)
            then(dve.tensor_tensor(s["b"], s["i0"], s["i1"], ALU.max))
            dve.tensor_tensor(s["t1"], s["first"], s["w1"], ALU.mult)
            then(dve.tensor_tensor(s["t2"], s["first"], s["w2"], ALU.mult))
            dve.tensor_tensor(s["w1"], s["w1"], s["t1"], ALU.subtract)
            then(dve.tensor_tensor(s["w2"], s["w2"], s["t2"], ALU.subtract))
            dve.tensor_tensor(wab[:, :, 0], s["w2"], s["t1"], ALU.add)
            dve.tensor_tensor(wab[:, :, 1], s["w1"], s["t2"], ALU.add).then_inc(wab_ok, 1)
            dve.tensor_scalar(s["a"], s["a"], float(E), None, ALU.add)
            then(dve.tensor_scalar(s["b"], s["b"], float(E - 1), None, ALU.add))
            then(dve.tensor_scalar(s["t2"], s["a"], -0.5, E - 1.5, ALU.mult, ALU.add))
            then(dve.tensor_tensor(s["t2"], s["t2"], s["a"], ALU.mult))
            then(dve.tensor_tensor(s["q"], s["t2"], s["b"], ALU.add))
            each_q = iota_q[:, :].unsqueeze(2).to_broadcast([P, PAIRS, B])
            then(dve.tensor_tensor(onehot[:, :, :], each_q, sm["q"][:, :].unsqueeze(1).to_broadcast([P, PAIRS, B]),
                                   ALU.is_equal))
            flat = "p q c -> p (q c)"
            then(dve.tensor_tensor_scan(rank[:, :, :].rearrange(flat), keep[:, :, :].rearrange(flat),
                                        onehot[:, :, :].rearrange(flat), 0.0, ALU.mult, ALU.add))
            dve.tensor_copy(row_count[:, :], rank[:, :, B - 1]).then_inc(count_ok, 1)
            dve.wait_ge(prefix_ps, 1)
            then(dve.tensor_scalar(tiles_i[:, :], bank[2][:, 0:PAIRS], float(P - 1), None, ALU.add))
            then(dve.tensor_scalar(tiles_i[:, :], tiles_i[:, :], 7, None, ALU.logical_shift_right))
            then(dve.tensor_copy(tiles_f[:, :], tiles_i[:, :]))
            then(dve.tensor_tensor_scan(tiles_end[:, :], ones_b[:, 0:PAIRS], tiles_f[:, :], 0.0, ALU.mult, ALU.add))
            then(dve.tensor_tensor(slot_base[:, :], tiles_end[:, :], tiles_f[:, :], ALU.subtract))
            then(dve.tensor_scalar(slot_base[:, :], slot_base[:, :], float(P), -1.0, ALU.mult, ALU.add))
            then(dve.tensor_tensor(slot_base[:, :], slot_base[:, :], bank[1][:, 0:PAIRS], ALU.add))
            then(dve.tensor_tensor(rank[:, :, :], rank[:, :, :],
                                   slot_base[:, :].unsqueeze(2).to_broadcast([P, PAIRS, B]), ALU.add))
            then(dve.tensor_tensor(rank[:, :, :], rank[:, :, :], onehot[:, :, :], ALU.mult))
            then(dve.tensor_reduce(s["slot"], rank[:, :, :].rearrange("p q c -> p c q"), AX.X, ALU.add))
            then(dve.tensor_copy(slot_i[:, :], s["slot"]))
            then(dve.tensor_scalar(part_i[:, :], slot_i[:, :], P - 1, None, ALU.bitwise_and))
            dve.tensor_copy(s["lo"], part_i[:, :])
            then(dve.tensor_scalar(slot_i[:, :], slot_i[:, :], 7, None, ALU.logical_shift_right))
            dve.tensor_copy(s["hi"], slot_i[:, :]).then_inc(acc_used, 1)
            dve.wait_ge(acc_used, 1)
            with dve.Fori(0, ROUNDS) as n:
                for c in range(WB):
                    if c >= 8:
                        dve.wait_ge(acc_ps, WB * n + (c - 7))
                    col = bass.ds(WB * n + c, 1)
                    dve.tensor_scalar(lo_hot[:, c % 8], iota_lo[:, :], sm["lo"][:, col],
                                      number[:, c:c + 1], ALU.is_equal, ALU.mult)
                    dve.tensor_scalar(hi_hot[:, c % 8], iota_hi[:, :], sm["hi"][:, col], None,
                                      ALU.is_equal).then_inc(hot_ok, 1)
                dve.wait_ge(acc_ps, WB * n + WB)
                dve.tensor_scalar(list_t[:, :], bank[3][:, 0:TILES], 0.0, round_base[:, bass.ds(n, 1)],
                                  ALU.is_gt, ALU.mult)
                dve.tensor_tensor(list_f[:, :], list_f[:, :], bank[3][:, 0:TILES], ALU.add).then_inc(acc_used, 1)
                dve.wait_ge(acc_used, n + 2)
                dve.tensor_tensor(list_f[:, :], list_f[:, :], list_t[:, :], ALU.add).then_inc(list_sum, 1)
                dve.wait_ge(list_sum, n + 1)
            then(dve.tensor_scalar(list_t[:, :], list_f[:, :], 0.0, float(PAD_ROW + 1), ALU.is_equal, ALU.mult))
            dve.scalar_tensor_tensor(list_i[:, :], list_f[:, :], -1.0, list_t[:, :], ALU.add,
                                     ALU.add).then_inc(list_ok, 1)
            then(dve.tensor_tensor(tq[:, :, :], iota_t[:, :].unsqueeze(2).to_broadcast([1, TILES, PAIRS]),
                                   tiles_end[0:1, :].unsqueeze(1).to_broadcast([1, TILES, PAIRS]), ALU.is_ge))
            then(dve.tensor_reduce(q_of[:, :], tq[:, :, :], AX.X, ALU.add))
            then(dve.tensor_scalar(q_of[:, :], q_of[:, :], float(PAIRS - 1), None, ALU.min))
            then(dve.tensor_tensor(tq[:, :, 0:E - 1], q_of[:, :].unsqueeze(2).to_broadcast([1, TILES, E - 1]),
                                   a_ends[:, :].unsqueeze(1).to_broadcast([1, TILES, E - 1]), ALU.is_ge))
            then(dve.tensor_reduce(ta[:, :], tq[:, :, 0:E - 1], AX.X, ALU.add))
            dve.tensor_copy(table[:, 0, :], ta[:, :]).then_inc(table_ok, 1)
            then(dve.tensor_scalar(tb[:, :], ta[:, :], 0.5, -(E - 1.5), ALU.mult, ALU.add))
            then(dve.tensor_tensor(tb[:, :], tb[:, :], ta[:, :], ALU.mult))
            then(dve.tensor_tensor(tb[:, :], tb[:, :], q_of[:, :], ALU.add))
            dve.wait_ge(shift_ps, 1)
            dve.tensor_tensor(b1T[:, :], b1T[:, :], bank[0][:, 0:E * HJ], ALU.add)
            dve.tensor_scalar(table[:, 1, :], tb[:, :], 1.0, None, ALU.add).then_inc(table_ok, 1)

            def step_b(i, k, active):
                if active[2]:
                    m, r = unit_of(i, k, 2)
                    u = RING * m + r
                    ge(dve, xh_ok, u + 1)
                    ge(dve, z_ps, 2 * u - 2)
                    dve.tensor_tensor(xl[:, r % 2], bank[4 + r % 2][:, 0:P], xh[:, r % 2],
                                      ALU.subtract).then_inc(xl_ok, 1)
                if active[4]:
                    m, r = unit_of(i, k, 4)
                    u = RING * m + r
                    y = bank[6 + r % 2]
                    ge(dve, y_ps, u + 1)
                    ge(dve, res_ok, u - 1)
                    dve.scalar_tensor_tensor(part[:, r % 2], y[:, 0:D], tile_row[:, r, 2 * D:2 * D + 1],
                                             tile_row[:, r, D:2 * D], ALU.mult, ALU.add).then_inc(part_ok, 1)
                    ge(dve, part_ok, u + 1)
                    ge(dve, out_st, 16 * (u - 1))
                    dve.scalar_tensor_tensor(result[:, r % 2], y[:, D:2 * D], tile_row[:, r, 2 * D + 1:2 * D + 2],
                                             part[:, r % 2], ALU.mult, ALU.add).then_inc(res_ok, 1)
                if active[3]:
                    m, r = unit_of(i, k, 3)
                    u = RING * m + r
                    ge(dve, y_ps, u - 1)
                    for n in range(2):
                        ge(dve, hid_ok, 2 * u + n + 1)
                        dve.tensor_copy(hid_h[:, r % 2, n], hid[:, n]).then_inc(hh_ok, 1)
                        ge(dve, hh_ok, 2 * u + n + 1)
                        dve.tensor_tensor(hid_l[:, r % 2, n], hid[:, n], hid_h[:, r % 2, n],
                                          ALU.subtract).then_inc(hl_ok, 1)

            steps(dve, TILES, 5, step_b)


def kernel(x, adj, L0_gnn_W, L0_gnn_b, L0_ffn_Wr, L0_ffn_br, L0_ffn_ln_g, L0_ffn_ln_b, L0_ffn_W1,
           L0_ffn_b1, L0_ffn_W2, L0_ffn_b2):
    import numpy as np
    import concourse.bacc as bacc
    from concourse.bass_utils import run_bass_kernel_spmd

    nc = bacc.Bacc("TRN2", target_bir_lowering=False, num_devices=1)
    given = {"x": x, "adj": adj, "gnn_w": L0_gnn_W, "gnn_b": L0_gnn_b, "wr": L0_ffn_Wr, "br": L0_ffn_br,
             "ln_g": L0_ffn_ln_g, "ln_b": L0_ffn_ln_b, "w1": L0_ffn_W1, "b1": L0_ffn_b1,
             "w2": L0_ffn_W2, "b2": L0_ffn_b2}
    arrays = {f"in_{n}": np.ascontiguousarray(a) for n, a in given.items()}
    args = [nc.dram_tensor(n, a.shape, mybir.dt.from_np(a.dtype), kind="ExternalInput").ap()
            for n, a in arrays.items()]
    out = nc.dram_tensor("out", x.shape, F32, kind="ExternalOutput").ap()
    gnn_moe(nc, *args, out)
    return run_bass_kernel_spmd(nc, [arrays], core_ids=[0]).results[0]["out"]
```

```python
from contextlib import ExitStack

import concourse.bass as bass
from concourse import mybir

F32, F16, BF16 = mybir.dt.float32, mybir.dt.float16, mybir.dt.bfloat16
I32, U32 = mybir.dt.int32, mybir.dt.uint32
ALU = mybir.AluOpType
ACT = mybir.ActivationFunctionType
AX = mybir.AxisListType

P = 128
EPS = 1e-5
TINY = 1.2e-38
WSCALE = 64.0
GPU = 4
WB = 16
RING_A, RING_B = 6, 6
W1_STAGE, W2_STAGE = 3, 4


def ge(eng, sem, count, most=None):
    if isinstance(count, int) and most is not None:
        count = min(count, most)
    if not isinstance(count, int) or count > 0:
        eng.wait_ge(sem, count)


class Time:

    def __init__(self, ring, i, k, active):
        self.ring, self.i, self.k, self.active = ring, i, k, active

    def unit(self, stage):
        m, r = self.i + (self.k - stage) // self.ring, (self.k - stage) % self.ring
        return self.ring * m + r, m, r


def steps(eng, ring, units, last_stage, step, start_round=None, after_first=None):
    def one(i, k, active):
        if k == 0 and start_round:
            start_round(i)
        step(Time(ring, i, k, active))

    def peeled(t):
        one(t // ring, t % ring, [0 <= t - s < units for s in range(last_stage + 1)])

    for t in range(2 * ring):
        peeled(t)
        if t == ring - 1 and after_first:
            after_first()
    with eng.Fori(2, units // ring) as i:
        for k in range(ring):
            one(i, k, [True] * (last_stage + 1))
    for t in range(units // ring * ring, units + last_stage):
        peeled(t)


class Offsets:

    def __init__(self, eng, name, table, most):
        self.eng, self.table, self.most = eng, table, most
        self.regs = [eng.alloc_register(f"{name}_offset{n}") for n in range(2 * (RING_B + 1))]

    def load(self, i):
        at = self.table[:, :, :].rearrange("o t n -> o (t n)")
        self.eng.load(self.regs, at[0:1, bass.ds(2 * RING_B * i, 2 * (RING_B + 1))])
        self.values = [self.eng.snap(reg, min_val=0, max_val=self.most) for reg in self.regs]

    def of(self, t, stage, n):
        return self.values[2 * (t.k - stage + W2_STAGE) + n]


def pick(ap, u):
    return ap[bass.ds(u, 1)].rearrange("o n c d -> (o n) c d")


def gnn_moe(nc, x, adj, gnn_w, gnn_b, wr, br, ln_g, ln_b, w1, b1, w2, b2, out):
    B, N, D = x.shape
    E, _, H = w1.shape
    HJ = H // P
    TOKENS = B * N
    UNITS = B // GPU
    UW = GPU * P
    PAIRS = E * (E - 1) // 2
    SUBS = 2
    TW = SUBS * P
    TILES = (TOKENS + PAIRS * (TW - 1)) // TW
    LISTS = TILES * SUBS
    ROW = 2 * D + 2
    PAD_ROW = TOKENS
    ROUNDS = B // WB
    BIAS = 2 * HJ
    assert N == P and D == P and B == P and H % TW == 0

    rows = nc.dram_tensor("token_rows", [TOKENS + 1, ROW], F32).ap()
    x_u = x.rearrange("(u c) n d -> u n c d", c=GPU)
    adj_u = adj.rearrange("(u c) n m -> u n c m", c=GPU)
    rows_u = rows[0:TOKENS, :].rearrange("(u c n) f -> u n c f", c=GPU, n=P)
    rows_c = rows[0:TOKENS, :].rearrange("(c n) f -> n c f", n=P)
    out_rows = out.rearrange("b n d -> (b n) d")

    with ExitStack() as ctx:
        def sb(name, shape, dt=F32, where=ctx):
            return where.enter_context(nc.sbuf_tensor(name, shape, dt))

        def sem(name):
            return ctx.enter_context(nc.semaphore(name))

        ident = sb("ident", [P, P])
        before = sb("before", [P, P], BF16)
        ones_b = sb("ones_b", [P, P], BF16)
        neg_half = sb("neg_half", [P, 4 * GPU])
        iota_e = sb("iota_e", [P, E])
        iota_q = sb("iota_q", [P, PAIRS])
        iota_lo = sb("iota_lo", [P, P], F16)
        iota_hi = sb("iota_hi", [P, LISTS], F16)
        number = sb("number", [P, WB])
        round_base = sb("round_base", [P, ROUNDS])
        gnn_w_in = sb("gnn_w_in", [P, P])
        gnn_wT = sb("gnn_wT", [P, P])
        gnn_b_row = sb("gnn_b_row", [1, P])
        wr_sb = sb("wr_sb", [P, E])
        br_all = sb("br_all", [P, E])
        ln_in = sb("ln_in", [2 * E, P])
        lnT = sb("lnT", [P, 2 * E])
        b1_in = sb("b1_in", [E * HJ, P])
        b2_in = sb("b2_in", [E, D])
        biases = sb("biases", [P, E, BIAS])
        w1_f = sb("w1_f", [P, E, H])
        w2_f = sb("w2_f", [P, E, H])
        w_s = sb("w_s", [P, E, H])
        w1_s = sb("w1_s", [P, E, 2, H], F16)
        w2_s = sb("w2_s", [P, E, 2, H], F16)

        zero_row = sb("zero_row", [1, ROW])
        keep = sb("keep", [P, PAIRS, B], BF16)
        iota_t = sb("iota_t", [1, TILES])
        a_ends = sb("a_ends", [1, E - 1])

        list_f = sb("list_f", [P, LISTS])

        logits = sb("logits", [P, B, E])
        list_i = sb("list_i", [P, LISTS], I32)
        pe_at = sb("pe_at", [1, TILES + 3 * RING_B, 2], I32)
        act_at = sb("act_at", [1, TILES + 3 * RING_B, 2], I32)

        with ExitStack() as a:
            x_in = sb("x_in", [P, RING_A, GPU, P], where=a)
            adj_in = sb("adj_in", [P, RING_A, GPU, P], where=a)
            pair_rows = sb("pair_rows", [P, RING_A, GPU, 2 * D], where=a)
            adjT = sb("adjT", [P, 3, UW], where=a)
            xd = sb("xd", [P, 2, GPU, P], where=a)
            aggT = sb("aggT", [P, 2, UW], where=a)
            degsum = sb("degsum", [1, 2, UW], where=a)
            relu = sb("relu", [P, 2, GPU, P], where=a)
            xnT = sb("xnT", [P, 2, UW], where=a)
            stats1 = sb("stats1", [P, 2, GPU, 6], where=a)
            stats2 = sb("stats2", [P, 2, GPU, 6], where=a)
            mv1 = sb("mv1", [P, 2, GPU, 2], where=a)
            mv2 = sb("mv2", [P, 2, GPU, 2], where=a)
            deg = sb("deg", [P, 2, GPU], where=a)
            z = sb("z", [P, 2, 4 * GPU], where=a)
            y = sb("y", [P, 2, 4 * GPU], where=a)
            dinv = sb("dinv", [P, RING_A, GPU], where=a)
            xs = sb("xs", [P, 2, GPU], where=a)
            nms = sb("nms", [P, 2, GPU], where=a)
            rt = sb("rt", [P, 2, GPU], where=a)
            ratio = sb("ratio", [P, RING_A, GPU], where=a)
        wab = sb("wab", [P, B, 2])
        wide = [sb(f"r_wide{n}", [P, B, E]) for n in range(2)]
        sm = {n: sb(f"r_{n}", [P, B]) for n in
              ("m1", "m2", "i0", "i1", "e", "w1", "w2", "first", "t1", "t2", "a", "b", "q",
               "slot", "lo", "hi")}
        slot_i = sb("slot_i", [P, B], I32)
        part_i = sb("part_i", [P, B], I32)
        onehot = sb("onehot", [P, PAIRS, B], BF16)
        rank = sb("rank", [P, PAIRS, B])
        row_count = sb("row_count", [P, PAIRS], BF16)
        tiles_i = sb("tiles_i", [P, PAIRS], I32)
        tiles_f = sb("tiles_f", [P, PAIRS])
        tiles_end = sb("tiles_end", [P, PAIRS])
        slot_base = sb("slot_base", [P, PAIRS])
        lo_hot = sb("lo_hot", [P, 8, P], F16)
        hi_hot = sb("hi_hot", [P, 8, LISTS], F16)
        list_t = sb("list_t", [P, LISTS])
        tq = sb("tq", [1, TILES, PAIRS], BF16)
        q_of = sb("q_of", [1, TILES])
        ta = sb("ta", [1, TILES])
        tb = sb("tb", [1, TILES])

        tile_row = sb("tile_row", [P, RING_B, SUBS, ROW])
        get_idx = sb("get_idx", [P, RING_B, SUBS], I32)
        put_idx = sb("put_idx", [P, RING_B, SUBS], I32)
        xh = sb("xh", [P, 2, TW], F16)
        xl = sb("xl", [P, 2, TW], F16)
        hid = sb("hid", [P, 2, HJ, TW])
        hid_h = sb("hid_h", [P, 2, 2, HJ, TW], F16)
        hid_l = sb("hid_l", [P, 2, 2, HJ, TW], F16)
        yT = sb("yT", [P, 2, 2, TW])
        part = sb("part", [P, 2, SUBS, D])
        result = sb("result", [P, RING_B, SUBS, D])

        bank = [ctx.enter_context(nc.psum_tensor(f"bank{n}", [P, 512], F32)) for n in range(8)]

        x_ld = [sem(f"x_ld{r}") for r in range(RING_A)]
        adj_ld = [sem(f"adj_ld{r}") for r in range(RING_A)]
        rows_st = [sem(f"rows_st{r}") for r in range(RING_A)]
        small_ld, w1_ld, w2_ld = sem("small_ld"), sem("w1_ld"), sem("w2_ld")
        pad_st, wab_st = sem("pad_st"), sem("wab_st")
        filled, consts = sem("filled"), sem("consts")
        prep_ps, prep_ok = sem("prep_ps"), sem("prep_ok")
        (stats_ok, mv_ok, ve_ok, z_ok, y_ok, dinv_ok, xs1_ok, xs_ok, xd_ok, adjT_ps, adjT_ok, agg_ps,
         agg_ok, dsum_ps, dsum_ok, gnn_ps, relu_ok, x1_ok, xn_ok, rt_ok, ratio_ok, xnT_ps,
         xnT_ok, lg_ps, lg_ok) = (sem("a_" + n) for n in (
             "stats", "mv", "ve", "z", "y", "dinv", "xs1", "xs", "xd", "adjT_ps", "adjT", "agg_ps", "agg",
             "dsum_ps", "dsum", "gnn_ps", "relu", "x1", "xn", "rt", "ratio", "xnT_ps", "xnT",
             "lg_ps", "lg"))
        link, gap_ok, exp_ok, wab_ok, count_ok, prefix_ps = (sem("r_" + n) for n in (
            "link", "gap", "exp", "wab", "count", "prefix_ps"))
        hot_ok, acc_ps, acc_used, list_sum, list_ok, table_ok, shift_ps = (sem("r_" + n) for n in (
            "hot", "acc_ps", "acc_used", "list_sum", "list", "table", "shift_ps"))
        scaled_ok, high_ok, low_ok = sem("w_scaled"), sem("w_high"), sem("w_low")
        row_ld = [sem(f"row_ld{r}") for r in range(RING_B)]
        out_st = [sem(f"out_st{r}") for r in range(RING_B)]
        (get_idx_ok, put_idx_ok, xT_ps, xh_ok, xl_ok, z_ps, hid_ok, hh_ok, hl_ok, y_ps, yT_ok, back_ps,
         part_ok, res_ok) = (sem("b_" + n) for n in (
             "get_idx", "put_idx", "xT_ps", "xh", "xl", "z_ps", "hid", "hh", "hl", "y_ps", "yT",
             "back_ps", "part", "res"))

        STAT2 = 5
        STEPS_A = UNITS + STAT2
        SMALL = 8
        FILLS, CONSTS = 5, 15
        block = ctx.enter_context(nc.Block())

        def rows_left(eng):
            for r in range(RING_A):
                eng.wait_ge(rows_st[r], 16 * ((UNITS - r + RING_A - 1) // RING_A))

        @block.sync
        def _(sp):
            def small(dst, src):
                sp.dma_start(dst, src).then_inc(small_ld, 16)

            small(gnn_w_in[:, :], gnn_w)
            small(gnn_b_row[:, :], gnn_b.rearrange("(a d) -> a d", a=1))
            small(wr_sb[:, :], wr)
            small(ln_in[0:E, :], ln_g)
            small(ln_in[E:2 * E, :], ln_b)
            small(b1_in[:, :], b1.rearrange("e (j p) -> (e j) p", p=P))
            small(b2_in[:, :], b2)
            small(br_all[:, :], br.partition_broadcast(P))

            def step(t):
                if t.active[0]:
                    u, m, r = t.unit(0)
                    ge(sp, x1_ok, u - RING_A + 1)
                    sp.dma_start(x_in[:, r], pick(x_u, u)).then_inc(x_ld[r], 16)
                    ge(sp, z_ok, u - RING_A + 1)
                    ge(sp, adjT_ps, u - RING_A + 1)
                    sp.dma_start(adj_in[:, r], pick(adj_u, u)).then_inc(adj_ld[r], 16)
                if t.active[7]:
                    u, m, r = t.unit(7)
                    ge(sp, xn_ok, u + 1)
                    sp.dma_start(pick(rows_u, u)[:, :, 0:2 * D], pair_rows[:, r]).then_inc(rows_st[r], 16)

            def experts_weights():
                sp.dma_start(w1_f[:, :, :], w1.rearrange("e p h -> p e h")).then_inc(w1_ld, 16)
                sp.dma_start(w2_f[:, :, :].rearrange("p e (j d) -> p (e j) d", j=HJ),
                             w2.rearrange("e (j p) d -> p (e j) d", p=P)).then_inc(w2_ld, 16)

            steps(sp, RING_A, UNITS, 7, step, after_first=experts_weights)
            sp.wait_ge(consts, CONSTS)
            sp.dma_start(rows[TOKENS:TOKENS + 1, :], zero_row[:, :]).then_inc(pad_st, 16)
            sp.wait_ge(wab_ok, 1)
            sp.dma_start(rows_c[:, :, 2 * D:2 * D + 2], wab[:, :, :]).then_inc(wab_st, 16)
            sp.wait_ge(pad_st, 16)
            sp.wait_ge(wab_st, 16)
            rows_left(sp)
            for r in range(RING_B):
                sp.wait_ge(out_st[r], 16 * SUBS * ((TILES - r + RING_B - 1) // RING_B))

        @block.gpsimd
        def _(pool):
            def fill(ap, value):
                pool.memset(ap, value).then_inc(filled, 1)

            def const(ins):
                ins.then_inc(consts, 1)

            fill(ident[:, :], 0.0)
            fill(before[:, :], 1.0)
            fill(keep[:, :, :], 1.0)
            fill(ones_b[:, :], 1.0)
            fill(neg_half[:, :], -0.5)
            pool.wait_ge(filled, FILLS)
            const(pool.affine_select(out=ident[:, :], in_=ident[:, :], compare_op=ALU.not_equal, fill=1.0,
                                     base=0, pattern=[[-1, P]], channel_multiplier=1))
            const(pool.affine_select(out=before[:, :], in_=before[:, :], compare_op=ALU.is_gt, fill=0.0,
                                     base=0, pattern=[[1, P]], channel_multiplier=-1))
            const(pool.affine_select(out=keep[:, :, :], in_=keep[:, :, :], compare_op=ALU.is_gt, fill=0.0,
                                     base=0, pattern=[[0, PAIRS], [1, B]], channel_multiplier=0))
            for ap, pattern, base, per_row in ((iota_e, [[1, E]], -E, 0), (iota_q, [[1, PAIRS]], 0, 0),
                                               (iota_lo, [[1, P]], 0, 0), (iota_hi, [[1, LISTS]], 0, 0),
                                               (number, [[P, WB]], 1, 1),
                                               (round_base, [[WB * P, ROUNDS]], 0, 0),
                                               (iota_t, [[1, TILES]], 0, 0)):
                const(pool.iota(ap[:, :], pattern=pattern, base=base, channel_multiplier=per_row,
                                allow_small_or_imprecise_dtypes=True))
            const(pool.memset(zero_row[:, :], 0.0))
            const(pool.memset(list_f[:, :], 0.0))
            const(pool.memset(pe_at[:, :, :], 0))
            const(pool.memset(act_at[:, :, :], 0))
            for a in range(E - 1):
                end = sum(E - 1 - n for n in range(a + 1))
                last = pool.memset(a_ends[:, a:a + 1], float(end))
            const(last)

            def step(t):
                if t.active[4]:
                    u, m, r = t.unit(4)
                    ge(pool, relu_ok, u + 1)
                    ge(pool, rows_st[r], 16 * m)
                    pool.tensor_tensor(pair_rows[:, r, :, D:2 * D], x_in[:, r], relu[:, r % 2],
                                       ALU.add).then_inc(x1_ok, 1)
                if t.active[0] or t.active[STAT2]:
                    u, m, r = t.unit(0)
                    ge(pool, z_ok, u + 1)
                    ge(pool, xs_ok, u - 1, UNITS)
                    ge(pool, xn_ok, u - STAT2 - 1)
                    ge(pool, ratio_ok, u - STAT2 - 1)
                    pool.tensor_tensor(y[:, r % 2], z[:, r % 2], neg_half[:, :], ALU.pow).then_inc(y_ok, 1)

            steps(pool, RING_A, UNITS, STAT2, step)

            for n, split in enumerate((w1_s, w2_s)):
                pool.wait_ge(high_ok, n + 1)
                pool.tensor_tensor(split[:, :, 1, :], w_s[:, :, :], split[:, :, 0, :],
                                   ALU.subtract).then_inc(low_ok, 1)

            pool.wait_ge(list_ok, 1)
            pool.wait_ge(wab_st, 16)
            pool.wait_ge(pad_st, 16)
            rows_left(pool)
            last_row, last_token = pool.to_reg(TOKENS), pool.to_reg(TOKENS - 1)

            def step_b(t):
                if t.active[1]:
                    u1, _, r1 = t.unit(1)
                    ge(pool, get_idx_ok, u1 + 1)
                    ge(pool, res_ok, u1 - RING_B + 1)
                if t.active[0]:
                    u, m, r = t.unit(0)
                    ge(pool, row_ld[r], 16 * SUBS * m)
                    pool.tensor_copy(get_idx[:, r, :], list_i[:, bass.ds(SUBS * u, SUBS)]).then_inc(get_idx_ok, 1)
                if t.active[1]:
                    for sub in range(SUBS):
                        pool.indirect_dma_start(
                            tile_row[:, r1, sub, :], None, rows[:, :],
                            bass.IndirectOffsetOnAxis(ap=get_idx[:, r1, sub:sub + 1].bitcast(U32), axis=0),
                            bounds_check=last_row, oob_is_err=False).then_inc(row_ld[r1], 16)
                pool.wait_ge(list_ok, 1)
                if t.active[6]:
                    u6, _, r6 = t.unit(6)
                    ge(pool, res_ok, u6 + 1)
                    ge(pool, put_idx_ok, u6 + 1)
                if t.active[5]:
                    u, m, r = t.unit(5)
                    ge(pool, out_st[r], 16 * SUBS * m)
                    pool.tensor_copy(put_idx[:, r, :], list_i[:, bass.ds(SUBS * u, SUBS)]).then_inc(put_idx_ok, 1)
                if t.active[6]:
                    for sub in range(SUBS):
                        pool.indirect_dma_start(
                            out_rows,
                            bass.IndirectOffsetOnAxis(ap=put_idx[:, r6, sub:sub + 1].bitcast(U32), axis=0),
                            result[:, r6, sub, :], None,
                            bounds_check=last_token, oob_is_err=False).then_inc(out_st[r6], 16)

            steps(pool, RING_B, TILES, 6, step_b)

        @block.scalar
        def _(act):
            def step(t):
                if t.active[2]:
                    u, m, r = t.unit(2)
                    ge(act, xs_ok, u + 1)
                    ge(act, agg_ps, u - 1)
                    for c in range(GPU):
                        last = act.activation(xd[:, r % 2, c], x_in[:, r, c], ACT.Identity,
                                              bias=nms[:, r % 2, c:c + 1], scale=xs[:, r % 2, c:c + 1])
                    last.then_inc(xd_ok, 1)
                if t.active[0]:
                    u, m, r = t.unit(0)
                    ge(act, adjT_ps, u + 1)
                    ge(act, agg_ps, u - 2)
                    ge(act, dsum_ps, u - 2)
                    act.activation(adjT[:, r % 3], bank[r % 2][:, :], ACT.Copy).then_inc(adjT_ok, 1)
                if t.active[3]:
                    u, m, r = t.unit(3)
                    ge(act, gnn_ps, u + 1)
                    ge(act, x1_ok, u - 1)
                    for c in range(GPU):
                        last = act.activation(relu[:, r % 2, c], bank[4 + r % 2][:, c * P:(c + 1) * P],
                                              ACT.Relu, scale=dinv[:, r, c:c + 1])
                    last.then_inc(relu_ok, 1)
                if t.active[2]:
                    u, m, r = t.unit(2)
                    ge(act, agg_ps, u + 1)
                    ge(act, gnn_ps, u - 1)
                    act.activation(aggT[:, r % 2], bank[2][:, :], ACT.Copy).then_inc(agg_ok, 1)
                    ge(act, dsum_ps, u + 1)
                    act.activation(degsum[:, r % 2], bank[3][0:1, :], ACT.Copy).then_inc(dsum_ok, 1)
                if t.active[7]:
                    u, m, r = t.unit(7)
                    ge(act, xnT_ps, u + 1)
                    ge(act, lg_ps, u - 1)
                    act.activation(xnT[:, r % 2], bank[6][:, :], ACT.Copy).then_inc(xnT_ok, 1)

            act.wait_ge(prep_ok, 3)
            steps(act, RING_A, UNITS, 7, step)

            act.wait_ge(w1_ld, 16)
            for e in range(E):
                last = act.activation(w_s[:, e, :], w1_f[:, e, :], ACT.Copy, scale=lnT[:, e:e + 1])
            last.then_inc(scaled_ok, 1)
            act.wait_ge(scaled_ok, 1)
            act.activation(w1_s[:, :, 0, :], w_s[:, :, :], ACT.Copy).then_inc(high_ok, 1)
            act.wait_ge(gap_ok, 1)
            act.activation(sm["e"][:, :], sm["t1"][:, :], ACT.Exp).then_inc(exp_ok, 1)
            act.wait_ge(low_ok, 1)
            act.wait_ge(w2_ld, 16)
            act.activation(w_s[:, :, :], w2_f[:, :, :], ACT.Copy, scale=WSCALE).then_inc(scaled_ok, 1)
            act.wait_ge(scaled_ok, 2)
            act.activation(w2_s[:, :, 0, :], w_s[:, :, :], ACT.Copy).then_inc(high_ok, 1)
            act.wait_ge(table_ok, 1)
            bias_of = biases[:, :, :].rearrange("p e n -> p (e n)")
            act_offset = Offsets(act, "act", act_at, BIAS * (E - 1))

            def expert(t, n):
                if t.active[3]:
                    u, m, r = t.unit(3)
                    e = act_offset.of(t, W1_STAGE, n)
                    ge(act, hl_ok, 2 * u + n - 1)
                    for j in range(HJ):
                        if j % 2 == 0:
                            ge(act, z_ps, 4 * u + (2 * n + j // 2 + 1))
                        last = act.activation(hid[:, n, j], bank[2 * n + j // 2][:, j % 2 * TW:(j % 2 + 1) * TW],
                                              ACT.Gelu, bias=bias_of[:, bass.ds(e + j, 1)], scale=1.0 / WSCALE)
                    last.then_inc(hid_ok, 1)
                if t.active[4]:
                    u, m, r = t.unit(4)
                    e = act_offset.of(t, W2_STAGE, n)
                    ge(act, y_ps, 2 * u + n + 1)
                    ge(act, back_ps, u - 1)
                    act.activation(yT[:, r % 2, n], bank[5 + n][:, 0:TW], ACT.Identity,
                                   bias=bias_of[:, bass.ds(e + HJ, 1)], scale=1.0 / WSCALE).then_inc(yT_ok, 1)

            def step_b(t):
                expert(t, 0)
                if t.active[2]:
                    u, m, r = t.unit(2)
                    ge(act, xT_ps, u + 1)
                    ge(act, z_ps, 4 * u - 4)
                    act.activation(xh[:, r % 2], bank[4][:, 0:TW], ACT.Copy).then_inc(xh_ok, 1)
                expert(t, 1)

            steps(act, RING_B, TILES, 4, step_b, start_round=act_offset.load)

        @block.tensor
        def _(pe):
            pe.wait_ge(small_ld, 16 * SMALL)
            pe.wait_ge(consts, 1)
            pe.transpose(bank[0][:, 0:P], gnn_w_in[:, :], ident[:, :])
            pe.transpose(bank[0][:, P:P + 2 * E], ln_in[:, :], ident[0:2 * E, 0:2 * E])
            pe.transpose(bank[0][:, 2 * P:2 * P + E * HJ], b1_in[:, :], ident[0:E * HJ, 0:E * HJ])
            pe.transpose(bank[0][:, 3 * P:3 * P + E], b2_in[:, :], ident[0:E, 0:E]).then_inc(prep_ps, 1)
            pe.wait_ge(prep_ok, 3)

            def step(t):
                if t.active[0]:
                    u, m, r = t.unit(0)
                    ge(pe, adj_ld[r], 16 * m + 16)
                    ge(pe, adjT_ok, u - 1)
                    for c in range(GPU):
                        last = pe.transpose(bank[r % 2][:, c * P:(c + 1) * P], adj_in[:, r, c], ident[:, :])
                    last.then_inc(adjT_ps, 1)
                if t.active[3]:
                    u, m, r = t.unit(3)
                    ge(pe, agg_ok, u + 1)
                    ge(pe, dsum_ok, u + 1)
                    ge(pe, relu_ok, u - 1)
                if t.active[8]:
                    u8, _, r8 = t.unit(8)
                    ge(pe, xnT_ok, u8 + 1)
                    ge(pe, lg_ok, u8)
                for c in range(GPU):
                    cols = slice(c * P, (c + 1) * P)
                    if t.active[3]:
                        o = bank[4 + r % 2][:, cols]
                        pe.matmul(o, aggT[:, r % 2, cols], gnn_wT[:, :], start=True, stop=False)
                        last = pe.matmul(o, degsum[:, r % 2, cols], gnn_b_row[:, :], start=False, stop=True)
                        if c == GPU - 1:
                            last.then_inc(gnn_ps, 1)
                    if t.active[8]:
                        last = pe.matmul(bank[7][:, c * E:(c + 1) * E], xnT[:, r8 % 2, cols], wr_sb[:, :],
                                         start=True, stop=True)
                        if c == GPU - 1:
                            last.then_inc(lg_ps, 1)
                if t.active[2]:
                    u, m, r = t.unit(2)
                    ge(pe, xd_ok, u + 1)
                    ge(pe, adjT_ok, u + 1)
                    ge(pe, agg_ok, u)
                    for c in range(GPU):
                        last = pe.matmul(bank[2][:, c * P:(c + 1) * P], xd[:, r % 2, c],
                                         adjT[:, r % 3, c * P:(c + 1) * P], start=True, stop=True)
                    last.then_inc(agg_ps, 1)
                    ge(pe, dsum_ok, u)
                    for c in range(GPU):
                        last = pe.matmul(bank[3][0:1, c * P:(c + 1) * P], dinv[:, r, c:c + 1],
                                         adjT[:, r % 3, c * P:(c + 1) * P], start=True, stop=True)
                    last.then_inc(dsum_ps, 1)
                if t.active[7]:
                    u, m, r = t.unit(7)
                    ge(pe, xn_ok, u + 1)
                    ge(pe, xnT_ok, u)
                    for c in range(GPU):
                        last = pe.transpose(bank[6][:, c * P:(c + 1) * P], pair_rows[:, r, c, 0:D], ident[:, :])
                    last.then_inc(xnT_ps, 1)

            steps(pe, RING_A, UNITS, 8, step)

            pe.wait_ge(w1_ld, 16)
            for n in range(E * HJ):
                e, j = divmod(n, HJ)
                last = pe.matmul(bank[0][:, n:n + 1], w1_f[:, e, j * P:(j + 1) * P], lnT[:, E + e:E + e + 1],
                                 start=True, stop=True)
            last.then_inc(shift_ps, 1)
            pe.wait_ge(count_ok, 1)
            pe.matmul(bank[1][:, 0:PAIRS], before[:, :], row_count[:, :], start=True, stop=True)
            pe.matmul(bank[2][:, 0:PAIRS], ones_b[:, :], row_count[:, :], start=True,
                      stop=True).then_inc(prefix_ps, 1)
            with pe.Fori(0, ROUNDS) as n:
                pe.wait_ge(acc_used, n + 1)
                for c in range(WB):
                    pe.wait_ge(hot_ok, WB * n + (c + 1))
                    last = pe.matmul(bank[3][:, 0:LISTS], lo_hot[:, c % 8], hi_hot[:, c % 8],
                                     start=(c == 0), stop=(c == WB - 1))
                    last.then_inc(acc_ps, 1)

            pe.wait_ge(low_ok, 2)
            pe.wait_ge(table_ok, 1)
            w1_at = w1_s[:, :, :, :].rearrange("p e l h -> p (e l h)")
            w2_at = w2_s[:, :, :, :].rearrange("p e l h -> p (e l h)")
            pe_offset = Offsets(pe, "pe", pe_at, 2 * H * (E - 1))

            def expert(t, n):
                if t.active[3]:
                    u, m, r = t.unit(3)
                    at = pe_offset.of(t, W1_STAGE, n)
                    ge(pe, xh_ok, u + 1)
                    ge(pe, xl_ok, u + 1)
                    ge(pe, hid_ok, 2 * u + n - 1)
                    for j in range(HJ):
                        o = bank[2 * n + j // 2][:, j % 2 * TW:(j % 2 + 1) * TW]
                        high = w1_at[:, bass.ds(at + j * P, P)]
                        pe.matmul(o, high, xh[:, r % 2], start=True, stop=False)
                        pe.matmul(o, high, xl[:, r % 2], start=False, stop=False)
                        last = pe.matmul(o, w1_at[:, bass.ds(at + (H + j * P), P)], xh[:, r % 2],
                                         start=False, stop=True)
                        if j % 2 == 1:
                            last.then_inc(z_ps, 1)
                if t.active[4]:
                    u, m, r = t.unit(4)
                    at = pe_offset.of(t, W2_STAGE, n)
                    ge(pe, yT_ok, 2 * u + n - 1)
                    ge(pe, hl_ok, 2 * u + n + 1)
                    o = bank[5 + n][:, 0:TW]
                    for j in range(HJ):
                        high = w2_at[:, bass.ds(at + j * P, P)]
                        pe.matmul(o, high, hid_h[:, r % 2, n, j], start=(j == 0), stop=False)
                        pe.matmul(o, high, hid_l[:, r % 2, n, j], start=False, stop=False)
                        last = pe.matmul(o, w2_at[:, bass.ds(at + (H + j * P), P)], hid_h[:, r % 2, n, j],
                                         start=False, stop=(j == HJ - 1))
                    last.then_inc(y_ps, 1)

            def step_b(t):
                expert(t, 0)
                if t.active[5]:
                    u, m, r = t.unit(5)
                    ge(pe, yT_ok, 2 * u + 2)
                    ge(pe, res_ok, u)
                    for sub in range(SUBS):
                        for n in range(2):
                            last = pe.transpose(bank[7][:, (SUBS * sub + n) * D:(SUBS * sub + n + 1) * D],
                                                yT[:, r % 2, n, sub * P:(sub + 1) * P], ident[:, :])
                    last.then_inc(back_ps, 1)
                if t.active[2]:
                    u, m, r = t.unit(2)
                    ge(pe, row_ld[r], 16 * SUBS * (m + 1))
                    ge(pe, xh_ok, u)
                    ge(pe, xl_ok, u)
                    for sub in range(SUBS):
                        last = pe.transpose(bank[4][:, sub * P:(sub + 1) * P], tile_row[:, r, sub, 0:D],
                                            ident[:, :])
                    last.then_inc(xT_ps, 1)
                expert(t, 1)

            steps(pe, RING_B, TILES, 5, step_b, start_round=pe_offset.load)

        @block.vector
        def _(dve):
            dve.wait_ge(prep_ps, 1)
            dve.tensor_copy(gnn_wT[:, :], bank[0][:, 0:P]).then_inc(prep_ok, 1)
            dve.tensor_scalar(lnT[:, 0:E], bank[0][:, P:P + E], WSCALE, None, ALU.mult)
            dve.tensor_copy(lnT[:, E:2 * E], bank[0][:, P + E:P + 2 * E]).then_inc(prep_ok, 1)
            dve.tensor_copy(biases[:, :, 0:HJ], bank[0][:, 2 * P:2 * P + E * HJ].rearrange(
                "p (e j) -> p e j", j=HJ))
            dve.tensor_copy(biases[:, :, HJ], bank[0][:, 3 * P:3 * P + E]).then_inc(prep_ok, 1)
            for n in range(2):
                dve.memset(z[:, n, :], 1.0)

            def step(t):
                norm1, norm2 = t.active[0], t.active[STAT2]
                u, m, r = t.unit(0)
                u2, _, r2 = t.unit(STAT2)
                if norm1:
                    ge(dve, x_ld[r], 16 * m + 16)
                    for c in range(GPU):
                        last = dve.bn_stats(stats1[:, r % 2, c], x_in[:, r, c])
                    ge(dve, adj_ld[r], 16 * m + 16)
                    last_stat = dve.tensor_reduce(deg[:, r % 2], adj_in[:, r], AX.X, ALU.add)
                if norm2:
                    ge(dve, x1_ok, u2 + 1)
                    for c in range(GPU):
                        last_stat = dve.bn_stats(stats2[:, r2 % 2, c], pair_rows[:, r2, c, D:2 * D])
                if norm1 or norm2:
                    last_stat.then_inc(stats_ok, 1)
                    ge(dve, stats_ok, u + 1)
                if t.active[9]:
                    u9, _, r9 = t.unit(9)
                    ge(dve, lg_ps, u9 + 1)
                    dve.tensor_tensor(logits[:, bass.ds(GPU * u9, GPU), :],
                                      bank[7][:, 0:GPU * E].rearrange("p (c e) -> p c e", e=E),
                                      ratio[:, r9].unsqueeze(2).to_broadcast([P, GPU, E]),
                                      ALU.mult).then_inc(lg_ok, 1)
                if norm1:
                    for c in range(GPU):
                        last = dve.bn_aggr(mv1[:, r % 2, c], stats1[:, r % 2, c])
                if norm2:
                    for c in range(GPU):
                        last = dve.bn_aggr(mv2[:, r2 % 2, c], stats2[:, r2 % 2, c])
                if norm1 or norm2:
                    last.then_inc(mv_ok, 1)
                    ge(dve, mv_ok, u + 1)
                    ge(dve, y_ok, u - 1)
                    if norm2:
                        last = dve.tensor_scalar(z[:, r % 2, 2 * GPU:3 * GPU], mv2[:, r2 % 2, :, 1], EPS, None,
                                                 ALU.add)
                        last.then_inc(ve_ok, 1)
                    if norm1:
                        dve.tensor_scalar(z[:, r % 2, 0:GPU], mv1[:, r % 2, :, 1], EPS, None, ALU.add)
                        last = dve.tensor_scalar(z[:, r % 2, GPU:2 * GPU], deg[:, r % 2], TINY, None, ALU.max)
                    if norm2:
                        ge(dve, ve_ok, u2 + 1)
                        last = dve.scalar_tensor_tensor(z[:, r % 2, 3 * GPU:], z[:, r % 2, 2 * GPU:3 * GPU], EPS,
                                                        mv2[:, r2 % 2, :, 1], ALU.mult, ALU.add)
                    last.then_inc(z_ok, 1)
                if t.active[1]:
                    u1, _, r1 = t.unit(1)
                    ge(dve, y_ok, u1 + 1)
                    ge(dve, relu_ok, u1 - RING_A + 1)
                    dve.scalar_tensor_tensor(dinv[:, r1], deg[:, r1 % 2], 0.0, y[:, r1 % 2, GPU:2 * GPU],
                                             ALU.is_gt, ALU.mult).then_inc(dinv_ok, 1)
                if t.active[STAT2 + 1]:
                    u5, _, r5 = t.unit(STAT2 + 1)
                    par = (r5 + STAT2) % 2
                    ge(dve, y_ok, u5 + STAT2 + 1)
                    dve.tensor_tensor(rt[:, r5 % 2], z[:, par, 3 * GPU:], y[:, par, 3 * GPU:],
                                      ALU.mult).then_inc(rt_ok, 1)
                if t.active[1]:
                    ge(dve, dinv_ok, u1 + 1)
                    ge(dve, xd_ok, u1 - 1)
                    dve.tensor_tensor(xs[:, r1 % 2], y[:, r1 % 2, 0:GPU], dinv[:, r1], ALU.mult).then_inc(xs1_ok, 1)
                if t.active[STAT2 + 1]:
                    ge(dve, rt_ok, u5 + 1)
                    dve.tensor_tensor(ratio[:, r5], rt[:, r5 % 2], y[:, par, 2 * GPU:3 * GPU],
                                      ALU.mult).then_inc(ratio_ok, 1)
                if t.active[1]:
                    ge(dve, xs1_ok, u1 + 1)
                    dve.scalar_tensor_tensor(nms[:, r1 % 2], mv1[:, r1 % 2, :, 0], -1.0, xs[:, r1 % 2], ALU.mult,
                                             ALU.mult).then_inc(xs_ok, 1)
                if t.active[STAT2 + 1]:
                    for c in range(GPU):
                        last = dve.tensor_scalar(pair_rows[:, r5, c, 0:D], pair_rows[:, r5, c, D:2 * D],
                                                 mv2[:, r5 % 2, c, 0:1], y[:, par, 3 * GPU + c:3 * GPU + c + 1],
                                                 ALU.subtract, ALU.mult)
                    last.then_inc(xn_ok, 1)

            steps(dve, RING_A, UNITS, 9, step)

            made = [0]

            def then(ins):
                made[0] += 1
                ins.then_inc(link, 1)
                dve.wait_ge(link, made[0])

            rows_left(dve)
            dve.wait_ge(consts, CONSTS)
            dve.wait_ge(lg_ok, UNITS)
            big0, big1 = (t[:, :, :] for t in wide)
            per_e = lambda ap: ap[:, :].unsqueeze(2).to_broadcast([P, B, E])
            per_c = lambda ap: ap[:, :].unsqueeze(1).to_broadcast([P, B, E])
            s = {n: t[:, :] for n, t in sm.items()}
            lg = logits[:, :, :]
            then(dve.tensor_tensor(lg, lg, per_c(br_all), ALU.add))
            then(dve.tensor_reduce(s["m1"], lg, AX.X, ALU.max))
            then(dve.tensor_tensor(big0, lg, per_e(sm["m1"]), ALU.is_equal))
            then(dve.tensor_tensor(big0, big0, per_c(iota_e), ALU.mult))
            then(dve.tensor_reduce(s["i0"], big0, AX.X, ALU.min))
            then(dve.tensor_tensor(big0, per_e(sm["i0"]), per_c(iota_e), ALU.is_equal))
            then(dve.scalar_tensor_tensor(big1, big0, -3e38, lg, ALU.mult, ALU.add))
            then(dve.tensor_reduce(s["w2"], big1, AX.X, ALU.max))
            dve.tensor_tensor(s["t1"], s["w2"], s["m1"], ALU.subtract).then_inc(gap_ok, 1)
            then(dve.tensor_tensor(big0, big1, per_e(sm["w2"]), ALU.is_equal))
            then(dve.tensor_tensor(big0, big0, per_c(iota_e), ALU.mult))
            then(dve.tensor_reduce(s["i1"], big0, AX.X, ALU.min))
            dve.wait_ge(exp_ok, 1)
            then(dve.tensor_scalar(s["t2"], s["e"], 1.0, None, ALU.add))
            then(dve.reciprocal(s["w1"], s["t2"]))
            then(dve.tensor_tensor(s["w2"], s["e"], s["w1"], ALU.mult))
            dve.tensor_tensor(s["first"], s["i0"], s["i1"], ALU.is_lt)
            dve.tensor_tensor(s["a"], s["i0"], s["i1"], ALU.min)
            then(dve.tensor_tensor(s["b"], s["i0"], s["i1"], ALU.max))
            dve.tensor_tensor(s["t1"], s["first"], s["w1"], ALU.mult)
            then(dve.tensor_tensor(s["t2"], s["first"], s["w2"], ALU.mult))
            dve.tensor_tensor(s["w1"], s["w1"], s["t1"], ALU.subtract)
            then(dve.tensor_tensor(s["w2"], s["w2"], s["t2"], ALU.subtract))
            dve.tensor_tensor(wab[:, :, 0], s["w2"], s["t1"], ALU.add)
            dve.tensor_tensor(wab[:, :, 1], s["w1"], s["t2"], ALU.add).then_inc(wab_ok, 1)
            dve.tensor_scalar(s["a"], s["a"], float(E), None, ALU.add)
            then(dve.tensor_scalar(s["b"], s["b"], float(E - 1), None, ALU.add))
            then(dve.tensor_scalar(s["t2"], s["a"], -0.5, E - 1.5, ALU.mult, ALU.add))
            then(dve.tensor_tensor(s["t2"], s["t2"], s["a"], ALU.mult))
            then(dve.tensor_tensor(s["q"], s["t2"], s["b"], ALU.add))
            each_q = iota_q[:, :].unsqueeze(2).to_broadcast([P, PAIRS, B])
            then(dve.tensor_tensor(onehot[:, :, :], each_q, sm["q"][:, :].unsqueeze(1).to_broadcast([P, PAIRS, B]),
                                   ALU.is_equal))
            flat = "p q c -> p (q c)"
            then(dve.tensor_tensor_scan(rank[:, :, :].rearrange(flat), keep[:, :, :].rearrange(flat),
                                        onehot[:, :, :].rearrange(flat), 0.0, ALU.mult, ALU.add))
            dve.tensor_copy(row_count[:, :], rank[:, :, B - 1]).then_inc(count_ok, 1)
            dve.wait_ge(prefix_ps, 1)
            then(dve.tensor_scalar(tiles_i[:, :], bank[2][:, 0:PAIRS], float(TW - 1), None, ALU.add))
            then(dve.tensor_scalar(tiles_i[:, :], tiles_i[:, :], TW.bit_length() - 1, None, ALU.logical_shift_right))
            then(dve.tensor_copy(tiles_f[:, :], tiles_i[:, :]))
            then(dve.tensor_tensor_scan(tiles_end[:, :], ones_b[:, 0:PAIRS], tiles_f[:, :], 0.0, ALU.mult, ALU.add))
            then(dve.tensor_tensor(slot_base[:, :], tiles_end[:, :], tiles_f[:, :], ALU.subtract))
            then(dve.tensor_scalar(slot_base[:, :], slot_base[:, :], float(TW), -1.0, ALU.mult, ALU.add))
            then(dve.tensor_tensor(slot_base[:, :], slot_base[:, :], bank[1][:, 0:PAIRS], ALU.add))
            then(dve.tensor_tensor(rank[:, :, :], rank[:, :, :],
                                   slot_base[:, :].unsqueeze(2).to_broadcast([P, PAIRS, B]), ALU.add))
            then(dve.tensor_tensor(rank[:, :, :], rank[:, :, :], onehot[:, :, :], ALU.mult))
            then(dve.tensor_reduce(s["slot"], rank[:, :, :].rearrange("p q c -> p c q"), AX.X, ALU.add))
            then(dve.tensor_copy(slot_i[:, :], s["slot"]))
            then(dve.tensor_scalar(part_i[:, :], slot_i[:, :], P - 1, None, ALU.bitwise_and))
            dve.tensor_copy(s["lo"], part_i[:, :])
            then(dve.tensor_scalar(slot_i[:, :], slot_i[:, :], P.bit_length() - 1, None, ALU.logical_shift_right))
            dve.tensor_copy(s["hi"], slot_i[:, :]).then_inc(acc_used, 1)
            dve.wait_ge(acc_used, 1)
            with dve.Fori(0, ROUNDS) as n:
                for c in range(WB):
                    if c >= 8:
                        dve.wait_ge(acc_ps, WB * n + (c - 7))
                    col = bass.ds(WB * n + c, 1)
                    dve.tensor_scalar(lo_hot[:, c % 8], iota_lo[:, :], sm["lo"][:, col],
                                      number[:, c:c + 1], ALU.is_equal, ALU.mult)
                    dve.tensor_scalar(hi_hot[:, c % 8], iota_hi[:, :], sm["hi"][:, col], None,
                                      ALU.is_equal).then_inc(hot_ok, 1)
                dve.wait_ge(acc_ps, WB * n + WB)
                dve.tensor_scalar(list_t[:, :], bank[3][:, 0:LISTS], 0.0, round_base[:, bass.ds(n, 1)],
                                  ALU.is_gt, ALU.mult)
                dve.tensor_tensor(list_f[:, :], list_f[:, :], bank[3][:, 0:LISTS], ALU.add).then_inc(acc_used, 1)
                dve.wait_ge(acc_used, n + 2)
                dve.tensor_tensor(list_f[:, :], list_f[:, :], list_t[:, :], ALU.add).then_inc(list_sum, 1)
                dve.wait_ge(list_sum, n + 1)
            then(dve.tensor_scalar(list_t[:, :], list_f[:, :], 0.0, float(PAD_ROW + 1), ALU.is_equal, ALU.mult))
            dve.scalar_tensor_tensor(list_i[:, :], list_f[:, :], -1.0, list_t[:, :], ALU.add,
                                     ALU.add).then_inc(list_ok, 1)
            then(dve.tensor_tensor(tq[:, :, :], iota_t[:, :].unsqueeze(2).to_broadcast([1, TILES, PAIRS]),
                                   tiles_end[0:1, :].unsqueeze(1).to_broadcast([1, TILES, PAIRS]), ALU.is_ge))
            then(dve.tensor_reduce(q_of[:, :], tq[:, :, :], AX.X, ALU.add))
            then(dve.tensor_scalar(q_of[:, :], q_of[:, :], float(PAIRS - 1), None, ALU.min))
            then(dve.tensor_tensor(tq[:, :, 0:E - 1], q_of[:, :].unsqueeze(2).to_broadcast([1, TILES, E - 1]),
                                   a_ends[:, :].unsqueeze(1).to_broadcast([1, TILES, E - 1]), ALU.is_ge))
            then(dve.tensor_reduce(ta[:, :], tq[:, :, 0:E - 1], AX.X, ALU.add))
            here = slice(W2_STAGE, W2_STAGE + TILES)
            dve.tensor_scalar(pe_at[:, here, 0], ta[:, :], float(2 * H), None, ALU.mult)
            dve.tensor_scalar(act_at[:, here, 0], ta[:, :], float(BIAS), None, ALU.mult)
            then(dve.tensor_scalar(tb[:, :], ta[:, :], 0.5, -(E - 1.5), ALU.mult, ALU.add))
            then(dve.tensor_tensor(tb[:, :], tb[:, :], ta[:, :], ALU.mult))
            then(dve.tensor_tensor(tb[:, :], tb[:, :], q_of[:, :], ALU.add))
            dve.wait_ge(shift_ps, 1)
            dve.tensor_tensor(biases[:, :, 0:HJ], biases[:, :, 0:HJ],
                              bank[0][:, 0:E * HJ].rearrange("p (e j) -> p e j", j=HJ), ALU.add)
            dve.tensor_scalar(pe_at[:, here, 1], tb[:, :], 1.0, float(2 * H), ALU.add, ALU.mult)
            dve.tensor_scalar(act_at[:, here, 1], tb[:, :], 1.0, float(BIAS), ALU.add,
                              ALU.mult).then_inc(table_ok, 1)

            def split(t, n):
                if t.active[3]:
                    u, m, r = t.unit(3)
                    ge(dve, y_ps, 2 * u + n - 3)
                    ge(dve, hid_ok, 2 * u + n + 1)
                    dve.tensor_copy(hid_h[:, r % 2, n], hid[:, n]).then_inc(hh_ok, 1)
                    ge(dve, hh_ok, 2 * u + n + 1)
                    dve.tensor_tensor(hid_l[:, r % 2, n], hid[:, n], hid_h[:, r % 2, n],
                                      ALU.subtract).then_inc(hl_ok, 1)

            def step_b(t):
                split(t, 0)
                if t.active[2]:
                    u, m, r = t.unit(2)
                    ge(dve, xh_ok, u + 1)
                    ge(dve, z_ps, 4 * u - 4)
                    dve.tensor_tensor(xl[:, r % 2], bank[4][:, 0:TW], xh[:, r % 2], ALU.subtract).then_inc(xl_ok, 1)
                if t.active[5]:
                    u, m, r = t.unit(5)
                    ge(dve, back_ps, u + 1)
                    for sub in range(SUBS):
                        o = bank[7][:, SUBS * sub * D:(SUBS * sub + 1) * D]
                        last = dve.scalar_tensor_tensor(part[:, r % 2, sub], o, tile_row[:, r, sub, 2 * D:2 * D + 1],
                                                        tile_row[:, r, sub, D:2 * D], ALU.mult, ALU.add)
                    last.then_inc(part_ok, 1)
                    ge(dve, part_ok, u + 1)
                    ge(dve, out_st[r], 16 * SUBS * m)
                    for sub in range(SUBS):
                        o = bank[7][:, (SUBS * sub + 1) * D:(SUBS * sub + 2) * D]
                        last = dve.scalar_tensor_tensor(result[:, r, sub], o,
                                                        tile_row[:, r, sub, 2 * D + 1:2 * D + 2],
                                                        part[:, r % 2, sub], ALU.mult, ALU.add)
                    last.then_inc(res_ok, 1)
                split(t, 1)

            steps(dve, RING_B, TILES, 5, step_b)


def kernel(x, adj, L0_gnn_W, L0_gnn_b, L0_ffn_Wr, L0_ffn_br, L0_ffn_ln_g, L0_ffn_ln_b, L0_ffn_W1,
           L0_ffn_b1, L0_ffn_W2, L0_ffn_b2):
    import numpy as np
    import concourse.bacc as bacc
    from concourse.bass_utils import run_bass_kernel_spmd

    nc = bacc.Bacc("TRN2", target_bir_lowering=False, num_devices=1)
    given = {"x": x, "adj": adj, "gnn_w": L0_gnn_W, "gnn_b": L0_gnn_b, "wr": L0_ffn_Wr, "br": L0_ffn_br,
             "ln_g": L0_ffn_ln_g, "ln_b": L0_ffn_ln_b, "w1": L0_ffn_W1, "b1": L0_ffn_b1,
             "w2": L0_ffn_W2, "b2": L0_ffn_b2}
    arrays = {f"in_{n}": np.ascontiguousarray(a) for n, a in given.items()}
    args = [nc.dram_tensor(n, a.shape, mybir.dt.from_np(a.dtype), kind="ExternalInput").ap()
            for n, a in arrays.items()]
    out = nc.dram_tensor("out", x.shape, F32, kind="ExternalOutput").ap()
    gnn_moe(nc, *args, out)
    return run_bass_kernel_spmd(nc, [arrays], core_ids=[0]).results[0]["out"]
```

```python
from contextlib import ExitStack

import concourse.bass as bass
from concourse import mybir

F32, F16, BF16 = mybir.dt.float32, mybir.dt.float16, mybir.dt.bfloat16
I32, U32 = mybir.dt.int32, mybir.dt.uint32
ALU = mybir.AluOpType
ACT = mybir.ActivationFunctionType
AX = mybir.AxisListType

P = 128
EPS = 1e-5
TINY = 1.2e-38
WSCALE = 64.0
GPU = 4
DVE_STEP = 5
ACT_XN = 2
WB = 16
RING_A, RING_B = 6, 6
W1_STAGE, W2_STAGE = 3, 4


def ge(eng, sem, count, most=None):
    if isinstance(count, int) and most is not None:
        count = min(count, most)
    if not isinstance(count, int) or count > 0:
        eng.wait_ge(sem, count)


class Time:

    def __init__(self, ring, i, k, active):
        self.ring, self.i, self.k, self.active = ring, i, k, active

    def unit(self, stage):
        m, r = self.i + (self.k - stage) // self.ring, (self.k - stage) % self.ring
        return self.ring * m + r, m, r


def steps(eng, ring, units, last_stage, step, start_round=None):
    def one(i, k, active):
        if k == 0 and start_round:
            start_round(i)
        step(Time(ring, i, k, active))

    def peeled(t):
        one(t // ring, t % ring, [0 <= t - s < units for s in range(last_stage + 1)])

    for t in range(2 * ring):
        peeled(t)
    with eng.Fori(2, units // ring) as i:
        for k in range(ring):
            one(i, k, [True] * (last_stage + 1))
    for t in range(units // ring * ring, units + last_stage):
        peeled(t)


class Offsets:

    def __init__(self, eng, name, table, most):
        self.eng, self.table, self.most = eng, table, most
        self.regs = [eng.alloc_register(f"{name}_offset{n}") for n in range(2 * (RING_B + 1))]

    def load(self, i):
        at = self.table[:, :, :].rearrange("o t n -> o (t n)")
        self.eng.load(self.regs, at[0:1, bass.ds(2 * RING_B * i, 2 * (RING_B + 1))])
        self.values = [self.eng.snap(reg, min_val=0, max_val=self.most) for reg in self.regs]

    def of(self, t, stage, n):
        return self.values[2 * (t.k - stage + W2_STAGE) + n]


def pick(ap, u):
    return ap[bass.ds(u, 1)].rearrange("o n c d -> (o n) c d")


def gnn_moe(nc, x, adj, gnn_w, gnn_b, wr, br, ln_g, ln_b, w1, b1, w2, b2, out):
    B, N, D = x.shape
    E, _, H = w1.shape
    HJ = H // P
    TOKENS = B * N
    UNITS = B // GPU
    UW = GPU * P
    PAIRS = E * (E - 1) // 2
    SUBS = 2
    TW = SUBS * P
    TILES = (TOKENS + PAIRS * (TW - 1)) // TW
    LISTS = TILES * SUBS
    ROW = 2 * D + 2
    PAD_ROW = TOKENS
    ROUNDS = B // WB
    FIRST = 2 * SUBS * RING_B
    ACT_STEPS = WB - WB // DVE_STEP
    LW = 104
    BIAS = 2 * HJ
    assert N == P and D == P and B == P and H % TW == 0

    rows = nc.dram_tensor("token_rows", [TOKENS + 1, ROW], F32).ap()
    x_u = x.rearrange("(u c) n d -> u n c d", c=GPU)
    adj_u = adj.rearrange("(u c) n m -> u n c m", c=GPU)
    rows_u = rows[0:TOKENS, :].rearrange("(u c n) f -> u n c f", c=GPU, n=P)
    rows_c = rows[0:TOKENS, :].rearrange("(c n) f -> n c f", n=P)
    out_rows = out.rearrange("b n d -> (b n) d")

    with ExitStack() as ctx:
        def sb(name, shape, dt=F32, where=ctx):
            return where.enter_context(nc.sbuf_tensor(name, shape, dt))

        def sem(name):
            return ctx.enter_context(nc.semaphore(name))

        ident = sb("ident", [P, P])
        before = sb("before", [P, P], BF16)
        ones_b = sb("ones_b", [P, P], BF16)
        neg_half = sb("neg_half", [P, 4 * GPU])
        iota_e = sb("iota_e", [P, B, E], BF16)
        ident_h = sb("ident_h", [P, P], F16)
        iota_lo = sb("iota_lo", [P, P], F16)
        iota_hi = sb("iota_hi", [P, LISTS + 1], F16)
        number = sb("number", [P, WB])
        round_base = sb("round_base", [P, ROUNDS])
        gnn_w_in = sb("gnn_w_in", [P, P])
        gnn_v = sb("gnn_v", [P, P])
        gnn_b_col = sb("gnn_b_col", [P, 1])
        gnn_u = sb("gnn_u", [P, 2])
        gnn_v_in = sb("gnn_v_in", [P, P])
        wr_sb = sb("wr_sb", [P, LW])
        br_all = sb("br_all", [P, E])
        ln_in = sb("ln_in", [2 * E, P])
        lnT = sb("lnT", [P, 2 * E])
        b1_in = sb("b1_in", [E * HJ, P])
        b2_in = sb("b2_in", [E, D])
        biases = sb("biases", [P, E, BIAS])
        w1_f = sb("w1_f", [P, E, H])
        w2_f = sb("w2_f", [P, E, H])
        w_s = sb("w_s", [P, E, H])
        w1_s = sb("w1_s", [P, E, 2, H], F16)
        w2_s = sb("w2_s", [P, E, 2, H], F16)
        gelu_first = sb("gelu_first", [1, 1])
        zero_row = sb("zero_row", [1, ROW])
        iota_q = sb("iota_q", [P, PAIRS, B], F16)
        keep = sb("keep", [P, PAIRS, B], F16)
        iota_t = sb("iota_t", [P, 1])
        a_ends = sb("a_ends", [P, E - 1])

        logits = sb("logits", [P, B, E])
        list_i = sb("list_i", [P, LISTS], I32)
        pe_at = sb("pe_at", [1, TILES + 3 * RING_B, 2], I32)
        act_at = sb("act_at", [1, TILES + 3 * RING_B, 2], I32)

        with ExitStack() as a:
            x_in = sb("x_in", [P, RING_A, GPU, P], where=a)
            adj_in = sb("adj_in", [P, RING_A, GPU, P], where=a)
            pair_rows = sb("pair_rows", [P, RING_A, GPU, 2 * D], where=a)
            adjT = sb("adjT", [P, 3, UW], where=a)
            xd = sb("xd", [P, 2, GPU, P], where=a)
            aggT = sb("aggT", [P, 2, UW], where=a)
            relu = sb("relu", [P, 2, GPU, P], where=a)
            xnT = sb("xnT", [P, 2, UW], where=a)
            stats1 = sb("stats1", [P, 2, GPU, 6], where=a)
            stats2 = sb("stats2", [P, 2, GPU, 6], where=a)
            mv1 = sb("mv1", [P, 2, GPU, 2], where=a)
            mv2 = sb("mv2", [P, 2, GPU, 2], where=a)
            deg = sb("deg", [P, 2, GPU], where=a)
            z = sb("z", [P, 2, 4 * GPU], where=a)
            y = sb("y", [P, 2, 4 * GPU], where=a)
            dinv = sb("dinv", [P, RING_A, GPU], where=a)
            xs = sb("xs", [P, 2, GPU], where=a)
            mr = sb("mr", [P, 2, GPU], where=a)
            nms = sb("nms", [P, 2, GPU], where=a)
            nm2 = sb("nm2", [P, 2, GPU], where=a)
            rt = sb("rt", [P, 2, GPU], where=a)
            ratio = sb("ratio", [P, RING_A, GPU], where=a)
        wab = sb("wab", [P, B, 2])
        wide = sb("r_wide", [P, B, E])
        mask = sb("mask", [P, B, E], BF16)
        sm = {n: sb(f"r_{n}", [P, B]) for n in
              ("m1", "i0", "i1", "e", "w1", "w2", "first", "t1", "t2", "t3", "a", "b",
               "slot", "lo", "hi", "step_bias")}
        slot_i = sb("slot_i", [P, B], I32)
        part_i = sb("part_i", [P, B], I32)
        q_h = sb("q_h", [P, B], F16)
        onehot = sb("onehot", [P, PAIRS, B], F16)
        slots = sb("slots", [P, PAIRS, B])
        row_count = sb("row_count", [P, PAIRS], BF16)
        tiles_i = sb("tiles_i", [P, PAIRS], I32)
        tiles_f = sb("tiles_f", [P, PAIRS])
        tiles_end = sb("tiles_end", [P, PAIRS])
        slot_base = sb("slot_base", [P, PAIRS])
        lo_hot = sb("lo_hot", [P, 8, P], F16)
        hi_step = sb("hi_step", [P, 8, LISTS + 1], F16)
        by_round = slots[:, :, :].rearrange("p q c -> p (q c)")
        sums = by_round[:, 0:ROUNDS * (LISTS + 1)].rearrange("p (n s) -> p n s", n=ROUNDS)
        based = onehot[:, :, :].rearrange("p q c -> p (q c)")[:, 0:ROUNDS * LISTS].rearrange(
            "p (n s) -> p n s", n=ROUNDS)
        found = by_round[:, ROUNDS * (LISTS + 1):ROUNDS * (2 * LISTS + 1)].rearrange("p (n s) -> p n s", n=ROUNDS)
        list_f = sb("list_f", [P, LISTS])
        list_t = sb("list_t", [P, LISTS])
        after = sb("after", [P, PAIRS])
        q_of = sb("q_of", [P, 1])
        ta = sb("ta", [P, 1])
        tb = sb("tb", [P, 1])

        with ExitStack() as early:
            rank = sb("rank", [P, PAIRS, B], F16, where=early)

        tile_row = sb("tile_row", [P, RING_B, SUBS, ROW])
        get_idx = sb("get_idx", [P, RING_B, SUBS], I32)
        put_idx = sb("put_idx", [P, RING_B, SUBS], I32)
        xh = sb("xh", [P, 2, TW], F16)
        xl = sb("xl", [P, 2, TW], F16)
        hid = sb("hid", [P, 2, HJ, TW])
        hid_h = sb("hid_h", [P, 2, 2, HJ, TW], F16)
        hid_l = sb("hid_l", [P, 2, 2, HJ, TW], F16)
        yT = sb("yT", [P, 2, 2, TW])
        part = sb("part", [P, 2, SUBS, D])
        result = sb("result", [P, RING_B, SUBS, D])

        bank = [ctx.enter_context(nc.psum_tensor(f"bank{n}", [P, 512], F32)) for n in range(8)]

        x_ld = [sem(f"x_ld{r}") for r in range(RING_A)]
        adj_ld = [sem(f"adj_ld{r}") for r in range(RING_A)]
        rows_st = [sem(f"rows_st{r}") for r in range(RING_A)]
        small_ld = sem("small_ld")
        w1_ld, w2_ld = ([sem(f"{n}_ld{half}") for half in range(2)] for n in ("w1", "w2"))
        pad_st, wab_st = sem("pad_st"), sem("wab_st")
        filled, consts = sem("filled"), sem("consts")
        wr_zero, gnn_ld, gnn_sum = sem("wr_zero"), sem("gnn_ld"), sem("gnn_sum")
        ident_ok, pool_ok = sem("ident_ok"), sem("pool_ok")
        prep_ps, prep_ok = sem("prep_ps"), sem("prep_ok")
        (stats_ok, mv_ok, ve_ok, z_ok, y_ok, dinv_ok, xs_ok, xd_ok, adjT_ps, adjT_ok, agg_ps,
         agg_ok, gnn_ps, relu_ok, x1_ok, nm2_ok, xn_ok, xn_act_ok, rt_ok, ratio_ok, xnT_ps,
         xnT_ok, lg_ps, lg_ok) = (sem("a_" + n) for n in (
             "stats", "mv", "ve", "z", "y", "dinv", "xs", "xd", "adjT_ps", "adjT", "agg_ps", "agg",
             "gnn_ps", "relu", "x1", "nm2", "xn", "xn_act", "rt", "ratio", "xnT_ps", "xnT",
             "lg_ps", "lg"))
        (link, pool_link, gap_ok, exp_ok, share_ok, wab_ok, count_ok, prefix_ps, tiles_ok, tiles_ps, bias_ok,
         rank_ok, rank_ps) = (
            sem("r_" + n) for n in ("link", "pool_link", "gap", "exp", "share", "wab", "count", "prefix_ps",
                                    "tiles", "tiles_ps", "bias", "rank", "rank_ps"))
        slot_ok, hot_ok, step_ok, acc_ps, acc_used, list_ok, table_ok, shift_ps = (sem("r_" + n) for n in (
            "slot", "hot", "step", "acc_ps", "acc_used", "list", "table", "shift_ps"))
        scaled_ok, high_ok, low_ok = sem("w_scaled"), sem("w_high"), sem("w_low")
        row_ld = [sem(f"row_ld{r}") for r in range(RING_B)]
        out_st = [sem(f"out_st{r}") for r in range(RING_B)]
        (get_idx_ok, put_idx_ok, xT_ps, xh_ok, xl_ok, z_ps, hid_ok, hh_ok, hl_ok, y_ps, yT_ok, back_ps,
         part_ok, res_ok) = (sem("b_" + n) for n in (
             "get_idx", "put_idx", "xT_ps", "xh", "xl", "z_ps", "hid", "hh", "hl", "y_ps", "yT",
             "back_ps", "part", "res"))

        STAT2 = 5
        SMALL = 6
        CONSTS = 13
        block = ctx.enter_context(nc.Block())

        def rows_left(eng):
            for r in range(RING_A):
                eng.wait_ge(rows_st[r], 16 * ((UNITS - r + RING_A - 1) // RING_A))

        @block.sync
        def _(sp):
            def step(t):
                if t.active[0]:
                    u, m, r = t.unit(0)
                    ge(sp, x1_ok, u - RING_A + 1)
                    sp.dma_start(x_in[:, r], pick(x_u, u)).then_inc(x_ld[r], 16)
                    ge(sp, z_ok, u - RING_A + 1)
                    ge(sp, adjT_ps, u - RING_A + 1)
                    sp.dma_start(adj_in[:, r], pick(adj_u, u)).then_inc(adj_ld[r], 16)
                if t.active[7]:
                    u, m, r = t.unit(7)
                    ge(sp, xn_ok, u + 1)
                    ge(sp, xn_act_ok, u + 1)
                    sp.dma_start(pick(rows_u, u)[:, :, 0:2 * D], pair_rows[:, r]).then_inc(rows_st[r], 16)
                if isinstance(t.i, int) and 0 <= t.unit(0)[0] - UNITS < 4:
                    experts_weights(t.unit(0)[0] - UNITS)

            w2_rows = w2.rearrange("e (j p) d -> p (e j) d", p=P)
            w2_cols = w2_f[:, :, :].rearrange("p e (j d) -> p (e j) d", j=HJ)

            def experts_weights(n):
                half = slice(n % 2 * (E // 2), (n % 2 + 1) * (E // 2))
                rows_of = slice(half.start * HJ, half.stop * HJ)
                if n < 2:
                    sp.dma_start(w1_f[:, half, :], w1.rearrange("e p h -> p e h")[:, half, :]).then_inc(w1_ld[n], 16)
                else:
                    sp.dma_start(w2_cols[:, rows_of], w2_rows[:, rows_of]).then_inc(w2_ld[n % 2], 16)

            steps(sp, RING_A, UNITS, 7, step)
            sp.wait_ge(consts, CONSTS)
            sp.dma_start(rows[TOKENS:TOKENS + 1, :], zero_row[:, :]).then_inc(pad_st, 16)
            sp.wait_ge(wab_ok, 1)
            sp.dma_start(rows_c[:, :, 2 * D:2 * D + 2], wab[:, :, :]).then_inc(wab_st, 16)
            sp.wait_ge(pad_st, 16)
            sp.wait_ge(wab_st, 16)
            rows_left(sp)
            for r in range(RING_B):
                sp.wait_ge(out_st[r], 16 * SUBS * ((TILES - r + RING_B - 1) // RING_B))

        @block.gpsimd
        def _(pool):
            pool.memset(wr_sb[:, :], 0.0).then_inc(wr_zero, 1)
            pool.memset(ident[:, :], 0.0).then_inc(ident_ok, 1)
            pool.wait_ge(ident_ok, 1)
            pool.affine_select(out=ident[:, :], in_=ident[:, :], compare_op=ALU.not_equal, fill=1.0, base=0,
                               pattern=[[-1, P]], channel_multiplier=1).then_inc(ident_ok, 1)
            pool.memset(neg_half[:, :], -0.5).then_inc(pool_ok, 1)
            pool.iota(iota_e[...], pattern=[[0, B], [1, E]], base=-E, channel_multiplier=0,
                      allow_small_or_imprecise_dtypes=True).then_inc(pool_ok, 1)
            pool.wait_ge(pool_ok, 2)

            def step(t):
                if t.active[4]:
                    u, m, r = t.unit(4)
                    ge(pool, relu_ok, u + 1)
                    ge(pool, rows_st[r], 16 * m)
                    pool.tensor_tensor(pair_rows[:, r, :, D:2 * D], x_in[:, r], relu[:, r % 2],
                                       ALU.add).then_inc(x1_ok, 1)
                if t.active[0] or t.active[STAT2]:
                    u, m, r = t.unit(0)
                    cols = slice(0 if t.active[0] else 2 * GPU, 4 * GPU if t.active[STAT2] else 2 * GPU)
                    ge(pool, z_ok, u + 1)
                    ge(pool, xs_ok, u - 1, UNITS)
                    ge(pool, xn_ok, u - STAT2 - 1)
                    ge(pool, xn_act_ok, u - STAT2 - 1)
                    ge(pool, ratio_ok, u - STAT2 - 1)
                    pool.tensor_tensor(y[:, r % 2, cols], z[:, r % 2, cols], neg_half[:, cols],
                                       ALU.pow).then_inc(y_ok, 1)

            steps(pool, RING_A, UNITS, STAT2, step)

            def const(ins):
                ins.then_inc(consts, 1)

            pool.memset(before[:, :], 1.0).then_inc(filled, 1)
            pool.memset(keep[:, :, :], 1.0).then_inc(filled, 1)
            pool.wait_ge(filled, 2)
            const(pool.affine_select(out=before[:, :], in_=before[:, :], compare_op=ALU.is_gt, fill=0.0,
                                     base=0, pattern=[[1, P]], channel_multiplier=-1))
            const(pool.memset(keep[:, :, 0], 0.0))
            const(pool.memset(ones_b[:, :], 1.0))
            for ap, pattern, base, per_row in ((iota_q, [[1, PAIRS], [0, B]], 0, 0),
                                               (iota_lo, [[1, P]], 0, 0), (iota_hi, [[1, LISTS + 1]], -1, 0),
                                               (number, [[P, WB]], 1, 1),
                                               (round_base, [[WB * P, ROUNDS]], 0, 0),
                                               (iota_t, [[1, 1]], 0, 1)):
                const(pool.iota(ap[...], pattern=pattern, base=base, channel_multiplier=per_row,
                                allow_small_or_imprecise_dtypes=True))
            const(pool.memset(zero_row[:, :], 0.0))
            const(pool.memset(pe_at[:, :, :], 0))
            const(pool.memset(act_at[:, :, :], 0))
            for a in range(E - 1):
                end = sum(E - 1 - n for n in range(a + 1))
                last = pool.memset(a_ends[:, a:a + 1], float(end))
            const(last)

            for n, split in enumerate((w1_s, w2_s)):
                pool.wait_ge(high_ok, n + 1)
                pool.tensor_tensor(split[:, :, 1, :], w_s[:, :, :], split[:, :, 0, :],
                                   ALU.subtract).then_inc(low_ok, 1)

            made = [0]

            def then(ins):
                made[0] += 1
                ins.then_inc(pool_link, 1)
                pool.wait_ge(pool_link, made[0])

            s = {n: t[:, :] for n, t in sm.items()}
            pool.wait_ge(share_ok, 1)
            then(pool.tensor_tensor(s["w2"], s["e"], s["w1"], ALU.mult))
            pool.tensor_tensor(s["t1"], s["first"], s["w1"], ALU.mult)
            then(pool.tensor_tensor(s["t2"], s["first"], s["w2"], ALU.mult))
            pool.tensor_tensor(s["w1"], s["w1"], s["t1"], ALU.subtract)
            then(pool.tensor_tensor(s["w2"], s["w2"], s["t2"], ALU.subtract))
            pool.tensor_tensor(wab[:, :, 0], s["w2"], s["t1"], ALU.add)
            pool.tensor_tensor(wab[:, :, 1], s["w1"], s["t2"], ALU.add).then_inc(wab_ok, 1)

            pool.wait_ge(list_ok, 1)
            pool.wait_ge(wab_st, 16)
            pool.wait_ge(pad_st, 16)
            rows_left(pool)
            last_row, last_token = pool.to_reg(TOKENS), pool.to_reg(TOKENS - 1)

            def step_b(t):
                if t.active[1]:
                    u1, _, r1 = t.unit(1)
                    ge(pool, get_idx_ok, u1 + 1)
                    ge(pool, res_ok, u1 - RING_B + 1)
                if t.active[0]:
                    u, m, r = t.unit(0)
                    ge(pool, row_ld[r], 16 * SUBS * m)
                    pool.tensor_copy(get_idx[:, r, :], list_i[:, bass.ds(SUBS * u, SUBS)]).then_inc(get_idx_ok, 1)
                if t.active[1]:
                    for sub in range(SUBS):
                        pool.indirect_dma_start(
                            tile_row[:, r1, sub, :], None, rows[:, :],
                            bass.IndirectOffsetOnAxis(ap=get_idx[:, r1, sub:sub + 1].bitcast(U32), axis=0),
                            bounds_check=last_row, oob_is_err=False).then_inc(row_ld[r1], 16)
                pool.wait_ge(list_ok, 1 if isinstance(t.i, int) and (t.i, t.k) < (1, RING_B - 1) else 2)
                if t.active[6]:
                    u6, _, r6 = t.unit(6)
                    ge(pool, res_ok, u6 + 1)
                    ge(pool, put_idx_ok, u6 + 1)
                if t.active[5]:
                    u, m, r = t.unit(5)
                    ge(pool, out_st[r], 16 * SUBS * m)
                    pool.tensor_copy(put_idx[:, r, :], list_i[:, bass.ds(SUBS * u, SUBS)]).then_inc(put_idx_ok, 1)
                if t.active[6]:
                    for sub in range(SUBS):
                        pool.indirect_dma_start(
                            out_rows,
                            bass.IndirectOffsetOnAxis(ap=put_idx[:, r6, sub:sub + 1].bitcast(U32), axis=0),
                            result[:, r6, sub, :], None,
                            bounds_check=last_token, oob_is_err=False).then_inc(out_st[r6], 16)

            steps(pool, RING_B, TILES, 6, step_b)

        @block.scalar
        def _(act):
            def small(dst, src, loaded):
                act.dma_start(dst, src).then_inc(loaded, 16)

            small(gnn_w_in[:, :], gnn_w, gnn_ld)
            small(gnn_b_col[:, :], gnn_b.rearrange("(d a) -> d a", a=1), gnn_ld)
            small(ln_in[0:E, :], ln_g, small_ld)
            small(ln_in[E:2 * E, :], ln_b, small_ld)
            small(b1_in[:, :], b1.rearrange("e (j p) -> (e j) p", p=P), small_ld)
            small(b2_in[:, :], b2, small_ld)
            small(br_all[:, :], br.partition_broadcast(P), small_ld)
            act.wait_ge(wr_zero, 1)
            small(wr_sb[:, 0:E], wr, small_ld)
            act.wait_ge(gnn_sum, 2)
            act.activation(gnn_v_in[:, :], gnn_w_in[:, :], ACT.Identity, bias=gnn_u[:, 1:2]).then_inc(gnn_sum, 1)
            act.wait_ge(ident_ok, 2)
            act.activation(ident_h[:, :], ident[:, :], ACT.Copy)
            act.wait_ge(prep_ps, 1)
            act.activation(gnn_v[:, :], bank[7][:, 0:P], ACT.Copy)
            act.activation(lnT[:, 0:E], bank[7][:, P:P + E], ACT.Copy, scale=WSCALE)
            act.activation(lnT[:, E:2 * E], bank[7][:, P + E:P + 2 * E], ACT.Copy)
            act.activation(biases[:, :, 0:HJ], bank[7][:, 2 * P:2 * P + E * HJ].rearrange(
                "p (e j) -> p e j", j=HJ), ACT.Copy)
            act.activation(biases[:, :, HJ], bank[7][:, 3 * P:3 * P + E], ACT.Copy).then_inc(prep_ok, 1)

            def step(t):
                if t.active[2]:
                    u, m, r = t.unit(2)
                    ge(act, xs_ok, u + 1)
                    ge(act, agg_ps, u - 1)
                    for c in range(GPU):
                        last = act.activation(xd[:, r % 2, c], x_in[:, r, c], ACT.Identity,
                                              bias=nms[:, r % 2, c:c + 1], scale=xs[:, r % 2, c:c + 1])
                    last.then_inc(xd_ok, 1)
                if t.active[0]:
                    u, m, r = t.unit(0)
                    ge(act, adjT_ps, u + 1)
                    ge(act, agg_ps, u - 2)
                    act.activation(adjT[:, r % 3], bank[r % 2][:, :], ACT.Copy).then_inc(adjT_ok, 1)
                if t.active[3]:
                    u, m, r = t.unit(3)
                    ge(act, gnn_ps, u + 1)
                    ge(act, x1_ok, u - 1)
                    for c in range(GPU):
                        last = act.activation(relu[:, r % 2, c], bank[4 + r % 2][:, c * P:(c + 1) * P],
                                              ACT.Relu, scale=dinv[:, r, c:c + 1])
                    last.then_inc(relu_ok, 1)
                if t.active[2]:
                    u, m, r = t.unit(2)
                    ge(act, agg_ps, u + 1)
                    ge(act, gnn_ps, u - 1)
                    act.activation(aggT[:, r % 2], bank[2][:, :], ACT.Copy).then_inc(agg_ok, 1)
                if t.active[STAT2 + 1]:
                    u, m, r = t.unit(STAT2 + 1)
                    par = (r + STAT2) % 2
                    ge(act, nm2_ok, u + 1)
                    for c in range(GPU - ACT_XN, GPU):
                        last = act.activation(pair_rows[:, r, c, 0:D], pair_rows[:, r, c, D:2 * D], ACT.Identity,
                                              bias=nm2[:, r % 2, c:c + 1],
                                              scale=y[:, par, 3 * GPU + c:3 * GPU + c + 1])
                    last.then_inc(xn_act_ok, 1)
                if t.active[7]:
                    u, m, r = t.unit(7)
                    ge(act, xnT_ps, u + 1)
                    ge(act, lg_ps, u - 1)
                    act.activation(xnT[:, r % 2], bank[6][:, :], ACT.Copy).then_inc(xnT_ok, 1)

            steps(act, RING_A, UNITS, 7, step)

            for half in w1_ld:
                act.wait_ge(half, 16)
            for e in range(E):
                last = act.activation(w_s[:, e, :], w1_f[:, e, :], ACT.Copy, scale=lnT[:, e:e + 1])
            last.then_inc(scaled_ok, 1)
            act.wait_ge(scaled_ok, 1)
            act.activation(w1_s[:, :, 0, :], w_s[:, :, :], ACT.Copy).then_inc(high_ok, 1)
            act.wait_ge(gap_ok, 1)
            act.activation(sm["e"][:, :], sm["t1"][:, :], ACT.Exp).then_inc(exp_ok, 1)
            act.wait_ge(low_ok, 1)
            for half in w2_ld:
                act.wait_ge(half, 16)
            act.activation(w_s[:, :, :], w2_f[:, :, :], ACT.Copy, scale=WSCALE).then_inc(scaled_ok, 1)
            act.wait_ge(scaled_ok, 2)
            act.activation(w2_s[:, :, 0, :], w_s[:, :, :], ACT.Copy).then_inc(high_ok, 1)
            act.wait_ge(slot_ok, 1)

            def steps_of_round(n):
                for c in range(WB):
                    if c % DVE_STEP != DVE_STEP - 1:
                        if c >= 8 or not isinstance(n, int):
                            act.wait_ge(acc_ps, WB * n + (c - 7))
                        act.activation(hi_step[:, c % 8], iota_hi[:, :], ACT.Sign,
                                       bias=sm["step_bias"][:, bass.ds(WB * n + c, 1)]).then_inc(step_ok, 1)

            steps_of_round(0)
            with act.Fori(1, ROUNDS) as n:
                steps_of_round(n)
            act.wait_ge(bias_ok, 1)
            act.activation(gelu_first[:, :], biases[0:1, 0, 0:1], ACT.Gelu)
            act.wait_ge(tiles_ps, 1)
            act.wait_ge(consts, CONSTS)
            for n in range(2):
                for at, size in ((pe_at, 2 * H), (act_at, BIAS)):
                    last = act.activation(at[:, W2_STAGE:W2_STAGE + TILES, n], bank[0][0:1, n * P:n * P + TILES],
                                          ACT.Copy, scale=float(size))
            last.then_inc(table_ok, 1)
            act.wait_ge(table_ok, 1)
            bias_of = biases[:, :, :].rearrange("p e n -> p (e n)")
            act_offset = Offsets(act, "act", act_at, BIAS * (E - 1))

            def expert(t, n):
                if t.active[3]:
                    u, m, r = t.unit(3)
                    e = act_offset.of(t, W1_STAGE, n)
                    ge(act, hl_ok, 2 * u + n - 1)
                    for j in range(HJ):
                        if j % 2 == 0:
                            ge(act, z_ps, 4 * u + (2 * n + j // 2 + 1))
                        last = act.activation(hid[:, n, j], bank[2 * n + j // 2][:, j % 2 * TW:(j % 2 + 1) * TW],
                                              ACT.Gelu, bias=bias_of[:, bass.ds(e + j, 1)], scale=1.0 / WSCALE)
                    last.then_inc(hid_ok, 1)
                if t.active[4]:
                    u, m, r = t.unit(4)
                    e = act_offset.of(t, W2_STAGE, n)
                    ge(act, y_ps, 2 * u + n + 1)
                    ge(act, back_ps, u - 1)
                    act.activation(yT[:, r % 2, n], bank[5 + n][:, 0:TW], ACT.Identity,
                                   bias=bias_of[:, bass.ds(e + HJ, 1)], scale=1.0 / WSCALE).then_inc(yT_ok, 1)

            def step_b(t):
                expert(t, 0)
                if t.active[2]:
                    u, m, r = t.unit(2)
                    ge(act, xT_ps, u + 1)
                    ge(act, z_ps, 4 * u - 4)
                    act.activation(xh[:, r % 2], bank[4][:, 0:TW], ACT.Copy).then_inc(xh_ok, 1)
                expert(t, 1)

            steps(act, RING_B, TILES, 4, step_b, start_round=act_offset.load)

        @block.tensor
        def _(pe):
            pe.wait_ge(small_ld, 16 * SMALL)
            pe.wait_ge(ident_ok, 2)
            pe.transpose(bank[7][:, P:P + 2 * E], ln_in[:, :], ident[0:2 * E, 0:2 * E])
            pe.transpose(bank[7][:, 2 * P:2 * P + E * HJ], b1_in[:, :], ident[0:E * HJ, 0:E * HJ])
            pe.transpose(bank[7][:, 3 * P:3 * P + E], b2_in[:, :], ident[0:E, 0:E])
            pe.wait_ge(gnn_sum, 3)
            pe.transpose(bank[7][:, 0:P], gnn_v_in[:, :], ident[:, :]).then_inc(prep_ps, 1)

            def step(t):
                if t.active[0]:
                    u, m, r = t.unit(0)
                    ge(pe, adj_ld[r], 16 * m + 16)
                    ge(pe, adjT_ok, u - 1)
                    for c in range(GPU):
                        last = pe.transpose(bank[r % 2][:, c * P:(c + 1) * P], adj_in[:, r, c], ident[:, :])
                    last.then_inc(adjT_ps, 1)
                if t.active[3]:
                    u, m, r = t.unit(3)
                    ge(pe, prep_ok, 1)
                    ge(pe, agg_ok, u + 1)
                    ge(pe, relu_ok, u - 1)
                    for c in range(GPU):
                        cols = slice(c * P, (c + 1) * P)
                        last = pe.matmul(bank[4 + r % 2][:, cols], aggT[:, r % 2, cols], gnn_v[:, :],
                                         start=True, stop=True)
                    last.then_inc(gnn_ps, 1)
                if t.active[2]:
                    u, m, r = t.unit(2)
                    ge(pe, xd_ok, u + 1)
                    ge(pe, adjT_ok, u + 1)
                    ge(pe, agg_ok, u)
                    for c in range(GPU):
                        last = pe.matmul(bank[2][:, c * P:(c + 1) * P], xd[:, r % 2, c],
                                         adjT[:, r % 3, c * P:(c + 1) * P], start=True, stop=True)
                    last.then_inc(agg_ps, 1)
                if t.active[8]:
                    u, m, r = t.unit(8)
                    ge(pe, xnT_ok, u + 1)
                    ge(pe, lg_ok, u - 1)
                    for c in range(GPU):
                        last = pe.matmul(bank[3 + 4 * (r % 2)][:, c * LW:(c + 1) * LW],
                                         xnT[:, r % 2, c * P:(c + 1) * P],
                                         wr_sb[:, :], start=True, stop=True)
                    last.then_inc(lg_ps, 1)
                if t.active[7]:
                    u, m, r = t.unit(7)
                    ge(pe, xn_ok, u + 1)
                    ge(pe, xn_act_ok, u + 1)
                    ge(pe, xnT_ok, u)
                    for c in range(GPU):
                        last = pe.transpose(bank[6][:, c * P:(c + 1) * P], pair_rows[:, r, c, 0:D], ident[:, :])
                    last.then_inc(xnT_ps, 1)

            steps(pe, RING_A, UNITS, 8, step)

            for half in w1_ld:
                pe.wait_ge(half, 16)
            for n in range(E * HJ):
                e, j = divmod(n, HJ)
                last = pe.matmul(bank[0][:, n:n + 1], w1_f[:, e, j * P:(j + 1) * P], lnT[:, E + e:E + e + 1],
                                 start=True, stop=True)
            last.then_inc(shift_ps, 1)
            pe.wait_ge(count_ok, 1)
            pe.matmul(bank[1][:, 0:PAIRS], before[:, :], row_count[:, :], start=True, stop=True)
            pe.matmul(bank[2][:, 0:PAIRS], ones_b[:, :], row_count[:, :], start=True,
                      stop=True).then_inc(prefix_ps, 1)
            pe.wait_ge(rank_ok, 1)
            for q in range(PAIRS):
                last = pe.matmul(bank[5][:, 0:B], ident_h[:, :], rank[:, q, :], start=(q == 0), stop=(q == PAIRS - 1))
            last.then_inc(rank_ps, 1)
            with pe.Fori(0, ROUNDS // 2) as n2:
                for half in range(2):
                    n = 2 * n2 + half
                    pe.wait_ge(acc_used, n + 1)
                    for c in range(WB):
                        pe.wait_ge(hot_ok, WB * n + (c + 1))
                        if c % DVE_STEP != DVE_STEP - 1:
                            pe.wait_ge(step_ok, ACT_STEPS * n + (c - c // DVE_STEP + 1))
                        pe.matmul(bank[3 + half][:, 0:LISTS + 1], lo_hot[:, c % 8], hi_step[:, c % 8],
                                  start=(c == 0), stop=(c == WB - 1)).then_inc(acc_ps, 1)
            pe.wait_ge(tiles_ok, 2)
            pe.matmul(bank[0][0:1, 0:P], ta[:, :], ident[:, :], start=True, stop=True)
            pe.matmul(bank[0][0:1, P:2 * P], tb[:, :], ident[:, :], start=True, stop=True).then_inc(tiles_ps, 1)

            pe.wait_ge(low_ok, 2)
            pe.wait_ge(table_ok, 1)
            w1_at = w1_s[:, :, :, :].rearrange("p e l h -> p (e l h)")
            w2_at = w2_s[:, :, :, :].rearrange("p e l h -> p (e l h)")
            pe_offset = Offsets(pe, "pe", pe_at, 2 * H * (E - 1))

            def expert(t, n):
                if t.active[3]:
                    u, m, r = t.unit(3)
                    at = pe_offset.of(t, W1_STAGE, n)
                    ge(pe, xh_ok, u + 1)
                    ge(pe, xl_ok, u + 1)
                    ge(pe, hid_ok, 2 * u + n - 1)
                    for j in range(HJ):
                        o = bank[2 * n + j // 2][:, j % 2 * TW:(j % 2 + 1) * TW]
                        high = w1_at[:, bass.ds(at + j * P, P)]
                        pe.matmul(o, high, xh[:, r % 2], start=True, stop=False)
                        pe.matmul(o, high, xl[:, r % 2], start=False, stop=False)
                        last = pe.matmul(o, w1_at[:, bass.ds(at + (H + j * P), P)], xh[:, r % 2],
                                         start=False, stop=True)
                        if j % 2 == 1:
                            last.then_inc(z_ps, 1)
                if t.active[4]:
                    u, m, r = t.unit(4)
                    at = pe_offset.of(t, W2_STAGE, n)
                    ge(pe, yT_ok, 2 * u + n - 1)
                    ge(pe, hl_ok, 2 * u + n + 1)
                    o = bank[5 + n][:, 0:TW]
                    for j in range(HJ):
                        high = w2_at[:, bass.ds(at + j * P, P)]
                        pe.matmul(o, high, hid_h[:, r % 2, n, j], start=(j == 0), stop=False)
                        pe.matmul(o, high, hid_l[:, r % 2, n, j], start=False, stop=False)
                        last = pe.matmul(o, w2_at[:, bass.ds(at + (H + j * P), P)], hid_h[:, r % 2, n, j],
                                         start=False, stop=(j == HJ - 1))
                    last.then_inc(y_ps, 1)

            def step_b(t):
                expert(t, 0)
                if t.active[5]:
                    u, m, r = t.unit(5)
                    ge(pe, yT_ok, 2 * u + 2)
                    ge(pe, res_ok, u)
                    for sub in range(SUBS):
                        for n in range(2):
                            last = pe.transpose(bank[7][:, (SUBS * sub + n) * D:(SUBS * sub + n + 1) * D],
                                                yT[:, r % 2, n, sub * P:(sub + 1) * P], ident[:, :])
                    last.then_inc(back_ps, 1)
                if t.active[2]:
                    u, m, r = t.unit(2)
                    ge(pe, row_ld[r], 16 * SUBS * (m + 1))
                    ge(pe, xh_ok, u)
                    ge(pe, xl_ok, u)
                    for sub in range(SUBS):
                        last = pe.transpose(bank[4][:, sub * P:(sub + 1) * P], tile_row[:, r, sub, 0:D],
                                            ident[:, :])
                    last.then_inc(xT_ps, 1)
                expert(t, 1)

            steps(pe, RING_B, TILES, 5, step_b, start_round=pe_offset.load)

        @block.vector
        def _(dve):
            dve.wait_ge(gnn_ld, 32)
            dve.tensor_reduce(gnn_u[:, 0:1], gnn_w_in[:, :], AX.X, ALU.add).then_inc(gnn_sum, 1)
            dve.wait_ge(gnn_sum, 1)
            dve.tensor_scalar(gnn_u[:, 1:2], gnn_b_col[:, :], gnn_u[:, 0:1], 1.0 / D, ALU.subtract,
                              ALU.mult).then_inc(gnn_sum, 1)

            def step(t):
                norm1, norm2 = t.active[0], t.active[STAT2]
                u, m, r = t.unit(0)
                u2, _, r2 = t.unit(STAT2)
                if norm1:
                    ge(dve, x_ld[r], 16 * m + 16)
                    for c in range(GPU):
                        last = dve.bn_stats(stats1[:, r % 2, c], x_in[:, r, c])
                if norm2:
                    ge(dve, x1_ok, u2 + 1)
                    for c in range(GPU):
                        last = dve.bn_stats(stats2[:, r2 % 2, c], pair_rows[:, r2, c, D:2 * D])
                if norm1 or norm2:
                    last.then_inc(stats_ok, 1)
                    ge(dve, stats_ok, u + 1)
                if norm1:
                    ge(dve, adj_ld[r], 16 * m + 16)
                    dve.tensor_reduce(deg[:, r % 2], adj_in[:, r], AX.X, ALU.add)
                if norm1:
                    for c in range(GPU):
                        last = dve.bn_aggr(mv1[:, r % 2, c], stats1[:, r % 2, c])
                if norm2:
                    for c in range(GPU):
                        last = dve.bn_aggr(mv2[:, r2 % 2, c], stats2[:, r2 % 2, c])
                if norm1 or norm2:
                    last.then_inc(mv_ok, 1)
                    ge(dve, mv_ok, u + 1)
                    ge(dve, y_ok, u - 1)
                    if norm2:
                        last = dve.tensor_scalar(z[:, r % 2, 2 * GPU:3 * GPU], mv2[:, r2 % 2, :, 1], EPS, None,
                                                 ALU.add)
                        last.then_inc(ve_ok, 1)
                    if norm1:
                        dve.tensor_scalar(z[:, r % 2, 0:GPU], mv1[:, r % 2, :, 1], EPS, None, ALU.add)
                        last = dve.tensor_scalar(z[:, r % 2, GPU:2 * GPU], deg[:, r % 2], TINY, None, ALU.max)
                    if norm2:
                        ge(dve, ve_ok, u2 + 1)
                        last = dve.scalar_tensor_tensor(z[:, r % 2, 3 * GPU:], z[:, r % 2, 2 * GPU:3 * GPU], EPS,
                                                        mv2[:, r2 % 2, :, 1], ALU.mult, ALU.add)
                    last.then_inc(z_ok, 1)
                if t.active[1]:
                    u1, _, r1 = t.unit(1)
                    ge(dve, y_ok, u1 + 1)
                    ge(dve, relu_ok, u1 - RING_A + 1)
                    dve.scalar_tensor_tensor(mr[:, r1 % 2], mv1[:, r1 % 2, :, 0], -1.0, y[:, r1 % 2, 0:GPU],
                                             ALU.mult, ALU.mult)
                    dve.scalar_tensor_tensor(dinv[:, r1], deg[:, r1 % 2], 0.0, y[:, r1 % 2, GPU:2 * GPU],
                                             ALU.is_gt, ALU.mult).then_inc(dinv_ok, 1)
                if t.active[STAT2 + 1]:
                    u5, _, r5 = t.unit(STAT2 + 1)
                    par = (r5 + STAT2) % 2
                    ge(dve, y_ok, u5 + STAT2 + 1)
                    dve.tensor_tensor(rt[:, r5 % 2], z[:, par, 3 * GPU:], y[:, par, 3 * GPU:],
                                      ALU.mult).then_inc(rt_ok, 1)
                    ge(dve, xn_act_ok, u5 - 1)
                    dve.scalar_tensor_tensor(nm2[:, r5 % 2], mv2[:, r5 % 2, :, 0], -1.0, y[:, par, 3 * GPU:],
                                             ALU.mult, ALU.mult).then_inc(nm2_ok, 1)
                if t.active[1]:
                    ge(dve, dinv_ok, u1 + 1)
                    ge(dve, xd_ok, u1 - 1)
                    dve.tensor_tensor(xs[:, r1 % 2], y[:, r1 % 2, 0:GPU], dinv[:, r1], ALU.mult)
                    dve.scalar_tensor_tensor(nms[:, r1 % 2], mr[:, r1 % 2], 1.0, dinv[:, r1], ALU.add,
                                             ALU.mult).then_inc(xs_ok, 1)
                if t.active[STAT2 + 1]:
                    ge(dve, rt_ok, u5 + 1)
                    dve.tensor_tensor(ratio[:, r5], rt[:, r5 % 2], y[:, par, 2 * GPU:3 * GPU],
                                      ALU.mult).then_inc(ratio_ok, 1)
                if t.active[STAT2 + 1]:
                    for c in range(GPU - ACT_XN):
                        last = dve.tensor_scalar(pair_rows[:, r5, c, 0:D], pair_rows[:, r5, c, D:2 * D],
                                                 mv2[:, r5 % 2, c, 0:1], y[:, par, 3 * GPU + c:3 * GPU + c + 1],
                                                 ALU.subtract, ALU.mult)
                    last.then_inc(xn_ok, 1)
                if t.active[8]:
                    u8, _, r8 = t.unit(8)
                    ge(dve, lg_ps, u8 + 1)
                    dve.tensor_tensor(logits[:, bass.ds(GPU * u8, GPU), :],
                                      bank[3 + 4 * (r8 % 2)][:, 0:GPU * LW].rearrange(
                                          "p (c l) -> p c l", l=LW)[:, :, 0:E],
                                      ratio[:, r8].unsqueeze(2).to_broadcast([P, GPU, E]),
                                      ALU.mult).then_inc(lg_ok, 1)

            steps(dve, RING_A, UNITS, 8, step)

            made = [0]

            def then(ins):
                made[0] += 1
                ins.then_inc(link, 1)
                dve.wait_ge(link, made[0])

            dve.wait_ge(pool_ok, 2)
            dve.wait_ge(lg_ok, UNITS)
            big, is_it, iota = wide[:, :, :], mask[:, :, :], iota_e[:, :, :]
            per_e = lambda ap: ap[:, :].unsqueeze(2).to_broadcast([P, B, E])
            per_c = lambda ap: ap[:, :].unsqueeze(1).to_broadcast([P, B, E])
            s = {n: t[:, :] for n, t in sm.items()}
            lg = logits[:, :, :]
            then(dve.tensor_tensor(lg, lg, per_c(br_all), ALU.add))
            then(dve.tensor_reduce(s["m1"], lg, AX.X, ALU.max))
            then(dve.tensor_tensor(is_it, lg, per_e(sm["m1"]), ALU.is_equal))
            then(dve.tensor_tensor(is_it, is_it, iota, ALU.mult))
            then(dve.tensor_reduce(s["i0"], is_it, AX.X, ALU.min))
            then(dve.tensor_tensor(is_it, per_e(sm["i0"]), iota, ALU.is_equal))
            then(dve.scalar_tensor_tensor(big, is_it, -3e38, lg, ALU.mult, ALU.add))
            then(dve.tensor_reduce(s["w2"], big, AX.X, ALU.max))
            dve.tensor_tensor(s["t1"], s["w2"], s["m1"], ALU.subtract).then_inc(gap_ok, 1)
            then(dve.tensor_tensor(is_it, big, per_e(sm["w2"]), ALU.is_equal))
            then(dve.tensor_tensor(is_it, is_it, iota, ALU.mult))
            then(dve.tensor_reduce(s["i1"], is_it, AX.X, ALU.min))
            dve.tensor_tensor(s["first"], s["i0"], s["i1"], ALU.is_lt)
            dve.tensor_tensor(s["a"], s["i0"], s["i1"], ALU.min)
            then(dve.tensor_tensor(s["b"], s["i0"], s["i1"], ALU.max))
            dve.tensor_scalar(s["a"], s["a"], float(E), None, ALU.add)
            then(dve.tensor_scalar(s["b"], s["b"], float(E - 1), None, ALU.add))
            then(dve.tensor_scalar(s["t3"], s["a"], -0.5, E - 1.5, ALU.mult, ALU.add))
            then(dve.tensor_tensor(s["t3"], s["t3"], s["a"], ALU.mult))
            then(dve.tensor_tensor(q_h[:, :], s["t3"], s["b"], ALU.add))
            dve.wait_ge(exp_ok, 1)
            then(dve.tensor_scalar(s["t2"], s["e"], 1.0, None, ALU.add))
            dve.reciprocal(s["w1"], s["t2"]).then_inc(share_ok, 1)
            dve.wait_ge(shift_ps, 1)
            dve.tensor_tensor(biases[:, :, 0:HJ], biases[:, :, 0:HJ],
                              bank[0][:, 0:E * HJ].rearrange("p (e j) -> p e j", j=HJ), ALU.add).then_inc(bias_ok, 1)
            rows_left(dve)
            dve.wait_ge(consts, CONSTS)
            then(dve.tensor_tensor(onehot[:, :, :], iota_q[:, :, :],
                                   q_h[:, :].unsqueeze(1).to_broadcast([P, PAIRS, B]), ALU.is_equal))
            flat = "p q c -> p (q c)"
            then(dve.tensor_tensor_scan(rank[:, :, :].rearrange(flat), keep[:, :, :].rearrange(flat),
                                        onehot[:, :, :].rearrange(flat), 0.0, ALU.mult, ALU.add))
            dve.tensor_copy(row_count[:, :], rank[:, :, B - 1]).then_inc(count_ok, 1)
            dve.wait_ge(count_ok, 1)
            dve.tensor_tensor(rank[:, :, :], rank[:, :, :], onehot[:, :, :], ALU.mult).then_inc(rank_ok, 1)
            dve.wait_ge(prefix_ps, 1)
            then(dve.tensor_scalar(tiles_i[:, :], bank[2][:, 0:PAIRS], float(TW - 1), None, ALU.add))
            then(dve.tensor_scalar(tiles_i[:, :], tiles_i[:, :], TW.bit_length() - 1, None, ALU.logical_shift_right))
            then(dve.tensor_copy(tiles_f[:, :], tiles_i[:, :]))
            dve.tensor_tensor_scan(tiles_end[:, :], ones_b[:, 0:PAIRS], tiles_f[:, :], 0.0, ALU.mult,
                                   ALU.add).then_inc(tiles_ok, 1)
            dve.wait_ge(tiles_ok, 1)
            then(dve.tensor_tensor(slot_base[:, :], tiles_end[:, :], tiles_f[:, :], ALU.subtract))
            then(dve.tensor_scalar(slot_base[:, :], slot_base[:, :], float(TW), -1.0, ALU.mult, ALU.add))
            then(dve.tensor_tensor(slot_base[:, :], slot_base[:, :], bank[1][:, 0:PAIRS], ALU.add))
            then(dve.tensor_tensor(slots[:, :, :], onehot[:, :, :],
                                   slot_base[:, :].unsqueeze(2).to_broadcast([P, PAIRS, B]), ALU.mult))
            then(dve.tensor_reduce(s["slot"], slots[:, :, :].rearrange("p q c -> p c q"), AX.X, ALU.add))
            dve.wait_ge(rank_ps, 1)
            then(dve.tensor_tensor(s["slot"], s["slot"], bank[5][:, 0:B], ALU.add))
            then(dve.tensor_copy(slot_i[:, :], s["slot"]))
            then(dve.tensor_scalar(part_i[:, :], slot_i[:, :], P - 1, None, ALU.bitwise_and))
            dve.tensor_copy(s["lo"], part_i[:, :]).then_inc(acc_used, 1)
            then(dve.tensor_scalar(slot_i[:, :], slot_i[:, :], P.bit_length() - 1, None, ALU.logical_shift_right))
            dve.tensor_copy(s["hi"], slot_i[:, :]).then_inc(acc_used, 1)
            dve.wait_ge(acc_used, 2)
            dve.tensor_scalar(s["step_bias"], s["hi"], -1.0, 0.5, ALU.mult, ALU.add).then_inc(slot_ok, 1)

            def hot(n):
                for c in range(WB):
                    if c >= 8 or not isinstance(n, int) or n > 0:
                        dve.wait_ge(acc_ps, WB * n + (c - 7))
                    col = bass.ds(WB * n + c, 1)
                    last = dve.tensor_scalar(lo_hot[:, c % 8], iota_lo[:, :], sm["lo"][:, col],
                                             number[:, c:c + 1], ALU.is_equal, ALU.mult)
                    if c % DVE_STEP == DVE_STEP - 1:
                        last = dve.tensor_scalar(hi_step[:, c % 8], iota_hi[:, :], sm["hi"][:, col], 2.0,
                                                 ALU.is_ge, ALU.mult)
                    last.then_inc(hot_ok, 1)

            def keep_sums(n, half):
                dve.wait_ge(acc_ps, WB * n + WB)
                dve.tensor_copy(sums[:, bass.ds(n, 1), :].rearrange("p o s -> p (o s)"),
                                bank[3 + half][:, 0:LISTS + 1]).then_inc(acc_used, 1)

            hot(0)
            with dve.Fori(0, ROUNDS // 2 - 1) as n2:
                for half in range(2):
                    hot(2 * n2 + (half + 1))
                    keep_sums(2 * n2 + half, half)
            hot(ROUNDS - 1)
            keep_sums(ROUNDS - 2, 0)
            keep_sums(ROUNDS - 1, 1)
            dve.wait_ge(acc_used, 2 + ROUNDS)

            def tiles_experts():
                then(dve.tensor_scalar(after[:, :], tiles_end[:, :], iota_t[:, :], None, ALU.is_le))
                then(dve.tensor_reduce(q_of[:, :], after[:, :], AX.X, ALU.add))
                then(dve.tensor_scalar(q_of[:, :], q_of[:, :], float(PAIRS - 1), None, ALU.min))
                then(dve.tensor_scalar(after[:, 0:E - 1], a_ends[:, :], q_of[:, :], None, ALU.is_le))
                then(dve.tensor_reduce(ta[:, :], after[:, 0:E - 1], AX.X, ALU.add))
                then(dve.tensor_scalar(tb[:, :], ta[:, :], 0.5, -(E - 1.5), ALU.mult, ALU.add))
                then(dve.tensor_tensor(tb[:, :], tb[:, :], ta[:, :], ALU.mult))
                then(dve.tensor_tensor(tb[:, :], tb[:, :], q_of[:, :], ALU.add))
                dve.tensor_scalar(tb[:, :], tb[:, :], 1.0, None, ALU.add).then_inc(tiles_ok, 1)

            for some in (slice(0, FIRST), slice(FIRST, LISTS)):
                nexts = slice(some.start + 1, some.stop + 1)
                then(dve.tensor_tensor(found[:, :, some], sums[:, :, nexts], sums[:, :, some], ALU.subtract))
                then(dve.scalar_tensor_tensor(based[:, :, some], found[:, :, some], 0.0,
                                              round_base[:, :].unsqueeze(2).to_broadcast(
                                                  [P, ROUNDS, some.stop - some.start]),
                                              ALU.is_gt, ALU.mult))
                then(dve.scalar_tensor_tensor(found[:, :, some], found[:, :, some], 0.5, based[:, :, some],
                                              ALU.mult, ALU.add))
                then(dve.tensor_reduce(list_f[:, some], found[:, :, some].rearrange("p n s -> p s n"), AX.X,
                                       ALU.add))
                then(dve.tensor_scalar(list_t[:, some], list_f[:, some], 0.0, float(PAD_ROW + 1), ALU.is_equal,
                                       ALU.mult))
                dve.scalar_tensor_tensor(list_i[:, some], list_f[:, some], -1.0, list_t[:, some], ALU.add,
                                         ALU.add).then_inc(list_ok, 1)
                if some.start == 0:
                    tiles_experts()

            def split(t, n):
                if t.active[3]:
                    u, m, r = t.unit(3)
                    ge(dve, y_ps, 2 * u + n - 3)
                    ge(dve, hid_ok, 2 * u + n + 1)
                    dve.tensor_copy(hid_h[:, r % 2, n], hid[:, n]).then_inc(hh_ok, 1)
                    ge(dve, hh_ok, 2 * u + n + 1)
                    dve.tensor_tensor(hid_l[:, r % 2, n], hid[:, n], hid_h[:, r % 2, n],
                                      ALU.subtract).then_inc(hl_ok, 1)

            def step_b(t):
                split(t, 0)
                if t.active[2]:
                    u, m, r = t.unit(2)
                    ge(dve, xh_ok, u + 1)
                    ge(dve, z_ps, 4 * u - 4)
                    dve.tensor_tensor(xl[:, r % 2], bank[4][:, 0:TW], xh[:, r % 2], ALU.subtract).then_inc(xl_ok, 1)
                if t.active[5]:
                    u, m, r = t.unit(5)
                    ge(dve, back_ps, u + 1)
                    for sub in range(SUBS):
                        o = bank[7][:, SUBS * sub * D:(SUBS * sub + 1) * D]
                        last = dve.scalar_tensor_tensor(part[:, r % 2, sub], o, tile_row[:, r, sub, 2 * D:2 * D + 1],
                                                        tile_row[:, r, sub, D:2 * D], ALU.mult, ALU.add)
                    last.then_inc(part_ok, 1)
                    ge(dve, part_ok, u + 1)
                    ge(dve, out_st[r], 16 * SUBS * m)
                    for sub in range(SUBS):
                        o = bank[7][:, (SUBS * sub + 1) * D:(SUBS * sub + 2) * D]
                        last = dve.scalar_tensor_tensor(result[:, r, sub], o,
                                                        tile_row[:, r, sub, 2 * D + 1:2 * D + 2],
                                                        part[:, r % 2, sub], ALU.mult, ALU.add)
                    last.then_inc(res_ok, 1)
                split(t, 1)

            steps(dve, RING_B, TILES, 5, step_b)


def kernel(x, adj, L0_gnn_W, L0_gnn_b, L0_ffn_Wr, L0_ffn_br, L0_ffn_ln_g, L0_ffn_ln_b, L0_ffn_W1,
           L0_ffn_b1, L0_ffn_W2, L0_ffn_b2):
    import numpy as np
    import concourse.bacc as bacc
    from concourse.bass_utils import run_bass_kernel_spmd

    nc = bacc.Bacc("TRN2", target_bir_lowering=False, num_devices=1)
    given = {"x": x, "adj": adj, "gnn_w": L0_gnn_W, "gnn_b": L0_gnn_b, "wr": L0_ffn_Wr, "br": L0_ffn_br,
             "ln_g": L0_ffn_ln_g, "ln_b": L0_ffn_ln_b, "w1": L0_ffn_W1, "b1": L0_ffn_b1,
             "w2": L0_ffn_W2, "b2": L0_ffn_b2}
    arrays = {f"in_{n}": np.ascontiguousarray(a) for n, a in given.items()}
    args = [nc.dram_tensor(n, a.shape, mybir.dt.from_np(a.dtype), kind="ExternalInput").ap()
            for n, a in arrays.items()]
    out = nc.dram_tensor("out", x.shape, F32, kind="ExternalOutput").ap()
    gnn_moe(nc, *args, out)
    return run_bass_kernel_spmd(nc, [arrays], core_ids=[0]).results[0]["out"]
```
